# Optimizing a Trainium2 kernel written in Bass

```python
import numpy as np
import jax
import jax.numpy as jnp

def _softmax(x, axis=-1):
    return jax.nn.softmax(x, axis=axis)

def _gelu(x):
    return jax.nn.gelu(x, approximate=True)

def _silu(x):
    return jax.nn.silu(x)

def _sigmoid(x):
    return jax.nn.sigmoid(x)

def _layernorm(x, axis=-1, eps=1e-05):
    m = jnp.mean(x, axis=axis, keepdims=True)
    v = jnp.var(x, axis=axis, keepdims=True)
    return (x - m) / jnp.sqrt(v + eps)

def _scatter_add(tgt, idx, src, axis=0):
    return tgt.at[idx].add(src)

def _segment_sum(src, seg, n):
    return jax.ops.segment_sum(src, seg, n)
kernel_name = 'mk_flamingo_gated_d2_seqx_r4_d131bd'

def setup_inputs(seed: int=0):
    np.random.seed(seed)
    _w = jnp.asarray

    def _rec_inputs():
        import jax
        import jax.numpy as jnp
        _rk = jax.random.key(seed)
        x = 7.22e-05 + 1 * jax.random.normal(jax.random.fold_in(_rk, 1), (32, 256, 256), jnp.float32)
        _lenS = 256 - jax.random.randint(jax.random.fold_in(_rk, 7), (32,), 0, max(1, 256 // 4) + 1, jnp.int32)
        _lenS2 = 77 - jax.random.randint(jax.random.fold_in(_rk, 8), (32,), 0, max(1, 77 // 4) + 1, jnp.int32)
        _ctx_1024P = jax.random.normal(jax.random.fold_in(_rk, 11), (32, 16, 256), jnp.float32)
        _ctx_1024c = jax.random.dirichlet(jax.random.fold_in(_rk, 511), 0.3 * jnp.ones((16,), jnp.float32), (32, 77))
        _ctx_1024t = jnp.einsum('bsk,bkd->bsd', _ctx_1024c, _ctx_1024P)
        _ctx_1024t = _ctx_1024t * jax.lax.rsqrt(jnp.mean(jnp.square(_ctx_1024t)) + 1e-12) * 0.953939
        ctx_1024 = 4.13588e-05 + 0.999923 * (_ctx_1024t + 0.3 * jax.random.normal(jax.random.fold_in(_rk, 611), (32, 77, 256), jnp.float32))
        _validS = jnp.arange(256)[None, :] < _lenS[:, None]
        _validS2 = jnp.arange(77)[None, :] < _lenS2[:, None]
        _causal = jnp.tril(jnp.ones((256, 256), dtype=bool))
        mask_1xSxS2_ff0 = jnp.where(jnp.ones((1, 256, 77), dtype=bool), 0.0, -1000000000.0).astype(jnp.float32)
        _g = jax.random.normal(jax.random.fold_in(_rk, 9001), (2, 2), jnp.float32)
        _g = jnp.sign(_g) * jnp.maximum(jnp.abs(_g), 1.0) + (_g == 0) * 1.0
        g_xattn = _g[0]
        g_ffn = _g[1]
        return (x, ctx_1024, mask_1xSxS2_ff0, g_xattn, g_ffn)
    x, ctx_1024, mask_1xSxS2_ff0, g_xattn, g_ffn = _rec_inputs()

    def _L0_xattn_setup():
        import jax, jax.numpy as jnp
        import numpy as np
        B, S, D_IN, D_MODEL = (4, 512, 256, 256)
        key = jax.random.key(seed)
        ks = jax.random.split(key, 8)
        glorot = np.sqrt(6.0 / (D_IN + D_MODEL))
        inp = {'q': jax.random.normal(ks[0], (B, S, D_IN), dtype=jnp.float32), 'k': jax.random.normal(ks[1], (B, S, D_IN), dtype=jnp.float32), 'v': jax.random.normal(ks[2], (B, S, D_IN), dtype=jnp.float32), 'mask': jnp.zeros((1, S, S), dtype=jnp.float32), 'kernel_q': jax.random.uniform(ks[3], (1, 1, D_IN, D_MODEL), jnp.float32, -glorot, glorot), 'kernel_k': jax.random.uniform(ks[4], (1, 1, D_IN, D_MODEL), jnp.float32, -glorot, glorot), 'kernel_v': jax.random.uniform(ks[5], (1, 1, D_IN, D_MODEL), jnp.float32, -glorot, glorot), 'bias_q': 0.05 * jax.random.normal(ks[6], (D_MODEL,), dtype=jnp.float32), 'bias_k': 0.05 * jax.random.normal(ks[7], (D_MODEL,), dtype=jnp.float32), 'bias_v': 0.05 * jax.random.normal(jax.random.fold_in(key, 7), (D_MODEL,), dtype=jnp.float32)}
        return inp
    _L0_xattn_all = _L0_xattn_setup()
    _L0_xattn_in = {k: v for k, v in _L0_xattn_all.items() if k in ('kernel_q', 'kernel_k', 'kernel_v', 'bias_q', 'bias_k', 'bias_v')}
    del _L0_xattn_all

    def _L0_ffn_setup():
        import jax, jax.numpy as jnp
        import numpy as np
        import math
        D_IN = 256
        FEATURES = (1024, 1024, 256)
        BATCH, SEQ = (8, 512)

        def _conn_dense(kernel_bool, x):
            w = jnp.where(kernel_bool, jnp.float32(1.0), jnp.float32(-1.0))
            return x @ w
        key = jax.random.key(seed)
        kx, kk0, kk1, kk2 = jax.random.split(key, 4)
        x = jax.random.normal(kx, (BATCH, SEQ, D_IN), dtype=jnp.float32)
        k0 = jax.random.randint(kk0, (2 * D_IN, FEATURES[0]), 0, 2).astype(jnp.bool_)
        k1 = jax.random.randint(kk1, (FEATURES[0], FEATURES[1]), 0, 2).astype(jnp.bool_)
        k2 = jax.random.randint(kk2, (FEATURES[1], FEATURES[2]), 0, 2).astype(jnp.bool_)
        s0 = jnp.asarray(1.0 / math.sqrt(2 * D_IN), dtype=jnp.float32)
        s1 = jnp.asarray(1.0 / math.sqrt(FEATURES[0]), dtype=jnp.float32)
        s2 = jnp.asarray(1.0 / math.sqrt(FEATURES[1]), dtype=jnp.float32)
        return {'x': x, 'k0': k0, 'k1': k1, 'k2': k2, 's0': s0, 's1': s1, 's2': s2}
    _L0_ffn_all = _L0_ffn_setup()
    _L0_ffn_in = {k: v for k, v in _L0_ffn_all.items() if k in ('k0', 'k1', 'k2', 's0', 's1', 's2')}
    del _L0_ffn_all

    def _L1_xattn_setup():
        import jax, jax.numpy as jnp
        import numpy as np
        N_HEAD = 16
        key = jax.random.key(seed)
        ks = jax.random.split(key, 5)
        b, l, d = (4, 512, 256)
        dh = d // N_HEAD
        return {'q': jax.random.normal(ks[0], (b, l, d), dtype=jnp.float32), 'kv': jax.random.normal(ks[1], (b, l, d), dtype=jnp.float32), 'Wq': jax.random.normal(ks[2], (d, d), dtype=jnp.float32) * 0.02, 'Wkv': jax.random.normal(ks[3], (2 * dh, d), dtype=jnp.float32) * 0.02, 'Wc': jax.random.normal(ks[4], (d, d), dtype=jnp.float32) * 0.02}
    _L1_xattn_all = _L1_xattn_setup()
    _L1_xattn_in = {k: v for k, v in _L1_xattn_all.items() if k in ('Wq', 'Wkv', 'Wc')}
    del _L1_xattn_all

    def _L1_ffn_setup():
        import jax, jax.numpy as jnp
        import numpy as np
        TOP_K = 8
        CAPACITY = 128

        def _silu(x):
            return x * jax.nn.sigmoid(x)
        key = jax.random.key(seed)
        ks = jax.random.split(key, 7)
        B, S, H, E, I, Is = (2, 256, 256, 64, 128, 512)
        s = 0.05
        return {'hidden_states': jax.random.normal(ks[0], (B, S, H), jnp.float32), 'gate_w': jax.random.normal(ks[1], (H, E), jnp.float32) * s, 'shared_gate_w': jax.random.normal(ks[2], (H, 1), jnp.float32) * s, 'shared_gate_up_w': jax.random.normal(ks[3], (H, 2 * Is), jnp.float32) * s, 'shared_down_w': jax.random.normal(ks[4], (Is, H), jnp.float32) * s, 'expert_gate_up_w': jax.random.normal(ks[5], (E, H, 2 * I), jnp.float32) * s, 'expert_down_w': jax.random.normal(ks[6], (E, I, H), jnp.float32) * s}
    _L1_ffn_all = _L1_ffn_setup()
    _L1_ffn_in = {k: v for k, v in _L1_ffn_all.items() if k in ('gate_w', 'shared_gate_w', 'shared_gate_up_w', 'shared_down_w', 'expert_gate_up_w', 'expert_down_w')}
    del _L1_ffn_all
    return {'x': x, 'ctx_1024': ctx_1024, 'mask_1xSxS2_ff0': mask_1xSxS2_ff0, 'g_xattn': g_xattn, 'g_ffn': g_ffn, 'L0_xattn_kernel_q': _L0_xattn_in['kernel_q'], 'L0_xattn_kernel_k': _L0_xattn_in['kernel_k'], 'L0_xattn_kernel_v': _L0_xattn_in['kernel_v'], 'L0_xattn_bias_q': _L0_xattn_in['bias_q'], 'L0_xattn_bias_k': _L0_xattn_in['bias_k'], 'L0_xattn_bias_v': _L0_xattn_in['bias_v'], 'L0_ffn_k0': _L0_ffn_in['k0'], 'L0_ffn_k1': _L0_ffn_in['k1'], 'L0_ffn_k2': _L0_ffn_in['k2'], 'L0_ffn_s0': _L0_ffn_in['s0'], 'L0_ffn_s1': _L0_ffn_in['s1'], 'L0_ffn_s2': _L0_ffn_in['s2'], 'L1_xattn_Wq': _L1_xattn_in['Wq'], 'L1_xattn_Wkv': _L1_xattn_in['Wkv'], 'L1_xattn_Wc': _L1_xattn_in['Wc'], 'L1_ffn_gate_w': _L1_ffn_in['gate_w'], 'L1_ffn_shared_gate_w': _L1_ffn_in['shared_gate_w'], 'L1_ffn_shared_gate_up_w': _L1_ffn_in['shared_gate_up_w'], 'L1_ffn_shared_down_w': _L1_ffn_in['shared_down_w'], 'L1_ffn_expert_gate_up_w': _L1_ffn_in['expert_gate_up_w'], 'L1_ffn_expert_down_w': _L1_ffn_in['expert_down_w']}

def reference(x, ctx_1024, mask_1xSxS2_ff0, g_xattn, g_ffn, L0_xattn_kernel_q, L0_xattn_kernel_k, L0_xattn_kernel_v, L0_xattn_bias_q, L0_xattn_bias_k, L0_xattn_bias_v, L0_ffn_k0, L0_ffn_k1, L0_ffn_k2, L0_ffn_s0, L0_ffn_s1, L0_ffn_s2, L1_xattn_Wq, L1_xattn_Wkv, L1_xattn_Wc, L1_ffn_gate_w, L1_ffn_shared_gate_w, L1_ffn_shared_gate_up_w, L1_ffn_shared_down_w, L1_ffn_expert_gate_up_w, L1_ffn_expert_down_w):
    import jax
    import jax.numpy as jnp

    def _L0_xattn_ref(q, k, v, mask, kernel_q, kernel_k, kernel_v, bias_q, bias_k, bias_v):
        import jax, jax.numpy as jnp
        import numpy as np
        B, S, D_IN, D_MODEL = (4, 512, 256, 256)
        Wq, Wk, Wv = (kernel_q[0, 0], kernel_k[0, 0], kernel_v[0, 0])
        qp = jax.nn.relu(jnp.einsum('bsd,de->bse', q, Wq) + bias_q)
        kp = jax.nn.relu(jnp.einsum('bsd,de->bse', k, Wk) + bias_k)
        vp = jax.nn.relu(jnp.einsum('bsd,de->bse', v, Wv) + bias_v)
        scores = jax.nn.relu(jnp.einsum('bqe,bke->bqk', qp, kp))
        dk = jnp.asarray(kp.shape[-1], dtype=scores.dtype)
        logits = scores / jnp.sqrt(dk) + mask
        out = jax.nn.relu(jnp.einsum('bqk,bke->bqe', logits, vp))
        return out

    def _L0_ffn_ref(x, k0, k1, k2, s0, s1, s2):
        import jax, jax.numpy as jnp
        import numpy as np
        import math
        D_IN = 256
        FEATURES = (1024, 1024, 256)
        BATCH, SEQ = (8, 512)

        def _conn_dense(kernel_bool, x):
            w = jnp.where(kernel_bool, jnp.float32(1.0), jnp.float32(-1.0))
            return x @ w
        h = jnp.concatenate([x, -x], axis=-1)
        h = s0 * _conn_dense(k0, h)
        h = jax.nn.relu(h) * 2
        h = s1 * _conn_dense(k1, h)
        h = jax.nn.relu(h) * 2
        h = s2 * _conn_dense(k2, h)
        return h

    def _L1_xattn_ref(q, kv, Wq, Wkv, Wc):
        import jax, jax.numpy as jnp
        import numpy as np
        N_HEAD = 16
        b, l, d = q.shape
        h = N_HEAD
        dh = d // h
        qp = jnp.einsum('bld,ed->ble', q, Wq)
        scores = jnp.einsum('bld,bmd->blm', qp, kv)
        idx = jnp.argmax(scores, axis=-1)
        mem = jnp.take_along_axis(kv, idx[..., None], axis=1)
        mkv = jnp.einsum('bld,ed->ble', mem, Wkv)
        mk, mv = jnp.split(mkv, 2, axis=-1)
        qh = qp.reshape(b, l, h, dh).transpose(0, 2, 1, 3)
        scale = 1.0 / np.sqrt(dh).astype(np.float32)
        logits = jnp.einsum('bhld,bmd->bhlm', qh, mk) * scale
        attn = jax.nn.softmax(logits, axis=-1)
        out = jnp.einsum('bhlm,bmd->bhld', attn, mv)
        out = out.transpose(0, 2, 1, 3).reshape(b, l, d)
        return jnp.einsum('bld,ed->ble', out, Wc)

    def _L1_ffn_ref(hidden_states, gate_w, shared_gate_w, shared_gate_up_w, shared_down_w, expert_gate_up_w, expert_down_w):
        import jax, jax.numpy as jnp
        import numpy as np
        TOP_K = 8
        CAPACITY = 128

        def _silu(x):
            return x * jax.nn.sigmoid(x)
        B, S, H = hidden_states.shape
        x = hidden_states.reshape(-1, H)
        T = x.shape[0]
        E = gate_w.shape[1]
        Is = shared_gate_up_w.shape[1] // 2
        I = expert_gate_up_w.shape[2] // 2
        gu = x @ shared_gate_up_w
        shared = _silu(gu[:, :Is]) * gu[:, Is:] @ shared_down_w
        shared = shared * jax.nn.sigmoid(x @ shared_gate_w)
        logits = x @ gate_w
        probs = jax.nn.softmax(logits.astype(jnp.float32), axis=-1)
        w, idx = jax.lax.top_k(probs, TOP_K)
        w = (w / jnp.sum(w, axis=-1, keepdims=True)).astype(x.dtype)
        e_flat = idx.reshape(-1)
        w_flat = w.reshape(-1)
        A = e_flat.shape[0]
        tok = jnp.arange(A) // TOP_K
        onehot = jax.nn.one_hot(e_flat, E, dtype=jnp.int32)
        pos = jnp.take_along_axis(jnp.cumsum(onehot, axis=0) - 1, e_flat[:, None], axis=1)[:, 0]
        slot = jnp.minimum(pos, CAPACITY)
        buf = jnp.zeros((E, CAPACITY + 1, H), x.dtype).at[e_flat, slot].set(x[tok])
        gu_e = jnp.einsum('ech,ehf->ecf', buf, expert_gate_up_w)
        act = _silu(gu_e[..., :I]) * gu_e[..., I:]
        out_e = jnp.einsum('eci,eih->ech', act, expert_down_w)
        y = out_e[e_flat, slot] * w_flat[:, None]
        y = jnp.where((pos < CAPACITY)[:, None], y, jnp.zeros_like(y))
        y = y.reshape(T, TOP_K, H).sum(axis=1)
        return (y + shared).reshape(B, S, H)
    x = x + jnp.tanh(g_xattn[0]) * _L0_xattn_ref(_layernorm(x, axis=-1), ctx_1024, ctx_1024, mask_1xSxS2_ff0, L0_xattn_kernel_q, L0_xattn_kernel_k, L0_xattn_kernel_v, L0_xattn_bias_q, L0_xattn_bias_k, L0_xattn_bias_v)
    x = x + jnp.tanh(g_ffn[0]) * _L0_ffn_ref(_layernorm(x, axis=-1), L0_ffn_k0, L0_ffn_k1, L0_ffn_k2, L0_ffn_s0, L0_ffn_s1, L0_ffn_s2)
    x = x + jnp.tanh(g_xattn[1]) * _L1_xattn_ref(_layernorm(x, axis=-1), ctx_1024, L1_xattn_Wq, L1_xattn_Wkv, L1_xattn_Wc)
    x = x + jnp.tanh(g_ffn[1]) * _L1_ffn_ref(_layernorm(x, axis=-1), L1_ffn_gate_w, L1_ffn_shared_gate_w, L1_ffn_shared_gate_up_w, L1_ffn_shared_down_w, L1_ffn_expert_gate_up_w, L1_ffn_expert_down_w)
    return x

_drawn_inputs = setup_inputs


def setup_inputs(seed=0):
    import zlib

    import numpy as np

    out = dict(_drawn_inputs(seed))
    spreads = {'g_ffn': (-1.0, 0.6)}
    factors = {'L0_xattn_bias_q': 8.0,
     'L0_xattn_bias_k': 8.0,
     'L1_xattn_Wq': 8.0,
     'L1_xattn_Wkv': 8.0,
     'L1_xattn_Wc': 8.0,
     'L1_ffn_gate_w': 8.0,
     'L1_ffn_shared_gate_w': 8.0,
     'L1_ffn_shared_gate_up_w': 8.0,
     'L1_ffn_shared_down_w': 8.0,
     'L1_ffn_expert_gate_up_w': 8.0,
     'L1_ffn_expert_down_w': 8.0}
    for name, (base, spread) in spreads.items():
        noise = np.random.default_rng([zlib.crc32(name.encode()), seed]).standard_normal(out[name].shape)
        drawn = base * np.exp(spread * noise) if base else spread * noise
        out[name] = jnp.asarray(drawn.astype(out[name].dtype))
    for name, factor in factors.items():
        out[name] = (out[name] * factor).astype(out[name].dtype)
    return out
```

```python
from contextlib import ExitStack

import numpy as np

import concourse.bass as bass
from concourse import mybir

F32 = mybir.dt.float32
F16 = mybir.dt.float16
BF16 = mybir.dt.bfloat16
I32 = mybir.dt.int32
U32 = mybir.dt.uint32
U8 = mybir.dt.uint8
ALU = mybir.AluOpType
ACT = mybir.ActivationFunctionType
AX = mybir.AxisListType.X

P = 128
NB, S, D = 32, 256, 256
S2 = 77
T2, C2 = S // P, D // P
F = 1024
FK = F // P
H, DH = 16, 16
HC = P // DH
HB = HC // 2
VW = DH + 1
E, IE, IS, CAP, TOPK = 64, 128, 512, 128, 8
SK = IS // P
NT = NB * S
XR = D + E
EPS = 1e-5
WS = 64.0
HS = 1.0 / 32
NEG = -1e30
XD = 4
GUESS = float(0x5F3759DF - (2 ** 23 + 2 ** 31) // 2)


def w(eng, sem, value):
    if isinstance(value, int) and value <= 0:
        return
    eng.wait_ge(sem, value)


class Many:

    def __init__(self, sem, per):
        self.sem, self.per = sem, per

    def nth(self, j, b):
        return b * self.per + j + 1


class Steps:

    def __init__(self, eng, sem, per):
        self.eng, self.sem, self.per = eng, sem, per

    def start(self, b):
        self.base, self.k = b * self.per, 0

    def did(self, ins):
        ins.then_inc(self.sem, 1)
        self.k += 1
        assert self.k <= self.per

    def wait(self):
        self.eng.wait_ge(self.sem, self.base + self.k)

    def end(self):
        assert self.k == self.per, (self.k, self.per)


def build(nc, x, ctxT, maskT, g_xattn, g_ffn, wq0, wk0, wv0, bq0, bk0, bv0, k0, k1, k2, s0, s1, s2,
          wqT1, wkvT1, wcT1, gates_w, sgu_w, sdown_w, egu_w, edown_w, out, xrows, table):
    es = ExitStack()
    with es:
        def sb(name, shape, dt=F32):
            return es.enter_context(nc.sbuf_tensor(name, shape, dt))

        def sem(name):
            return es.enter_context(nc.semaphore(name))

        def sems(name, n):
            return [sem(f"{name}{i}") for i in range(n)]

        def many(name, per):
            return Many(sem(name), per)

        bank = [es.enter_context(nc.psum_tensor(f"bank{i}", [P, 512], F32)) for i in range(2)]
        ps_lg = es.enter_context(nc.psum_tensor("ps_lg", [P, 2, 512], F32))
        ps_pt0 = es.enter_context(nc.psum_tensor("ps_pt0", [P, 512], F32))
        ps_m = es.enter_context(nc.psum_tensor("ps_m", [P, 512], F32))
        ps_tr = es.enter_context(nc.psum_tensor("ps_tr", [P, 512], F32))
        ps_yo = es.enter_context(nc.psum_tensor("ps_yo", [P, 512], F32))
        ps_pt = [ps_pt0, ps_yo]
        ps_eg = [ps_tr, ps_m]

        def two(ap):
            return ap[:, :].rearrange("p (a n) -> p a n", a=2)

        ident = sb("ident", [P, P])
        ones16 = sb("ones16", [P, P], F16)
        before16 = sb("before16", [P, P], F16)
        row0 = sb("row0", [P, P], BF16)
        iota_k = sb("iota_k", [P, S2])
        ebase = sb("ebase", [P, E])
        headmask = sb("headmask", [P, HC])
        epsc = sb("epsc", [P, 1])
        threehalf = sb("threehalf", [P, T2])
        tokf = sb("tokf", [P, T2])
        toki = sb("toki", [P, T2], I32)
        sent = sb("sent", [E, CAP], I32)
        sc = sb("sc", [P, 16])
        G0X, F0, G1X, G1F = (sc[:, i:i + 1] for i in range(4))
        raw = sb("raw", [P, 7])
        tg = sb("tg", [P, 4])
        sg = sb("sg", [P, 2])
        ab = sb("ab", [P, 2])
        dve_pad = sb("dve_pad", [P, 16])
        pool_pad = sb("pool_pad", [P, 8])
        stage = sb("stage", [P, 2048])
        stage32 = sb("stage32", [P, 2048], I32)
        stage8 = stage32[:, :].bitcast(U8)
        wq_h, wq_l = sb("wq_h", [P, C2, D], F16), sb("wq_l", [P, C2, D], F16)
        wk_h, wk_l = sb("wk_h", [P, C2, D], F16), sb("wk_l", [P, C2, D], F16)
        VN = D + DH
        wv_h, wv_l = sb("wv_h", [P, C2, VN], F16), sb("wv_l", [P, C2, VN], F16)
        wkr_h, wkr_l = sb("wkr_h", [P, C2, P], F16), sb("wkr_l", [P, C2, P], F16)
        wp_h, wp_l = sb("wp_h", [P, C2, D], F16), sb("wp_l", [P, C2, D], F16)
        wc_h, wc_l = sb("wc_h", [P, C2, D], F16), sb("wc_l", [P, C2, D], F16)
        gw_h, gw_l = sb("gw_h", [P, C2, E + 1], F16), sb("gw_l", [P, C2, E + 1], F16)
        gu_h, gu_l = sb("gu_h", [P, C2, 2 * IS], F16), sb("gu_l", [P, C2, 2 * IS], F16)
        dn_h, dn_l = sb("dn_h", [P, SK, D], F16), sb("dn_l", [P, SK, D], F16)
        wb0 = sb("wb0", [P, C2, F], F16)
        wb1 = sb("wb1", [P, FK, F], F16)
        wb2 = sb("wb2", [P, FK, D], F16)
        bqk = sb("bqk", [P, 2, C2])
        bv = sb("bv", [P, D])
        mT = sb("mT", [S2, S])
        x0 = sb("x0", [P, T2, D])
        ctx = sb("ctx", [P, C2, S2])
        ctx_h, ctx_l = sb("ctx_h", [P, C2, P], F16), sb("ctx_l", [P, C2, P], F16)
        xn = [sb(f"xn{i}", [P, T2, D]) for i in range(3)]
        xt_h = [sb(f"xt{i}_h", [P, C2, S], F16) for i in range(4)]
        xt_l = [sb(f"xt{i}_l", [P, C2, S], F16) for i in range(4)]
        LN_SIZE = (1, 2, 1)
        stats = [sb(f"stats{g}", [P, T2 * k, 6]) for g, k in enumerate(LN_SIZE)]
        mv = [sb(f"mv{g}", [P, T2 * k, 2]) for g, k in enumerate(LN_SIZE)]
        nt = [sb(f"nt{g}", [P, 2, T2 * k]) for g, k in enumerate(LN_SIZE)]
        rs_g = [sb(f"rs{g}", [P, T2 * k]) for g, k in enumerate(LN_SIZE)]
        nb_g = [sb(f"nb{g}", [P, T2 * k]) for g, k in enumerate(LN_SIZE)]
        rs, nb = ([v[0][:, :], v[1][:, 0:T2], v[1][:, T2:2 * T2], v[2][:, :]] for v in (rs_g, nb_g))
        q32 = sb("q32", [P, C2, S])
        kp32 = sb("kp32", [P, C2, P])
        v32 = sb("v32", [S2, D])
        v32r = sb("v32r", [S2, D])
        vp32 = sb("vp32", [S2, DH])
        kr32 = sb("kr32", [P, S2])
        s32 = sb("s32", [S2, S])
        l32 = sb("l32", [S2, S])
        o32 = sb("o32", [P, T2, D])
        x1 = sb("x1", [P, T2, D])
        x1_kept = sb("x1_kept", [P, T2, D])
        h0_h, h0_l = sb("h0_h", [P, FK, S], F16), sb("h0_l", [P, FK, S], F16)
        h1_h, h1_l = sb("h1_h", [P, FK, S], F16), sb("h1_l", [P, FK, S], F16)
        x2 = sb("x2", [P, T2, D])
        cx_h, cx_l = sb("cx_h", [P, C2, S2], F16), sb("cx_l", [P, C2, S2], F16)
        kr_h, kr_l = sb("kr_h", [P, S2], F16), sb("kr_l", [P, S2], F16)
        kb_h, kb_l = sb("kb_h", [P, HC, S2], F16), sb("kb_l", [P, HC, S2], F16)
        vpc = sb("vpc", [S2, DH])
        qp_h, qp_l = sb("qp_h", [P, C2, S], F16), sb("qp_l", [P, C2, S], F16)
        am8 = sb("am8", [P, T2, 8])
        ami = sb("ami", [P, T2, 8], U32)
        amf = sb("amf", [P, T2])
        hot = sb("hot", [P, T2, S2], F16)
        mrow = sb("mrow", [P, HB, S2], BF16)
        cnt = sb("cnt", [S2, 1])
        vc = sb("vc", [S2, DH])
        vc_h, vc_l = sb("vc_h", [S2, VW], F16), sb("vc_l", [S2, VW], F16)
        rmax = sb("rmax", [P, HC])
        z = sb("z", [P, HC, S2])
        p32 = sb("p32", [P, HC, S2])
        pt_h, pt_l = sb("pt_h", [S2, HC, P], F16), sb("pt_l", [S2, HC, P], F16)
        rden = sb("rden", [P, HC])
        att = sb("att", [P, T2, D])
        at_h, at_l = sb("at_h", [P, C2, S], F16), sb("at_l", [P, C2, S], F16)
        x3 = sb("x3", [P, T2, D])
        xr = sb("xr", [P, T2, XR])
        th = sb("th", [P, IS // P, S])
        ga = sb("ga", [P, 4, S])
        ac = sb("ac", [P, SK, S])
        ac_h, ac_l = sb("ac_h", [P, SK, S], F16), sb("ac_l", [P, SK, S], F16)
        lt8 = sb("lt8", [P, T2, 8])
        ltm = sb("ltm", [P, T2])
        ex = sb("ex", [P, T2, E])
        e8 = sb("e8", [P, T2, 8])
        es8 = sb("es8", [P, T2])
        er8 = sb("er8", [P, T2])
        erp = sb("erp", [P, T2, E])
        chosen = sb("chosen", [P, T2, E], F16)
        sgt = sb("sgt", [P, T2])
        sgc = sb("sgc", [P, T2])
        carry = sb("carry", [P, E])
        pos = sb("pos", [P, T2, E])
        kept = sb("kept", [P, T2, E])
        key = sb("key", [P, T2, E])
        val = sb("val", [P, T2, E])
        v8 = sb("v8", [P, T2, 8])
        slot = sb("slot", [P, T2, 8], I32)
        x4 = sb("x4", [P, T2, D])
        slots_row = sb("slots_row", [E, CAP], I32)
        slots_f = sb("slots_f", [E, CAP])
        ids = sb("ids", [P, E], I32)
        gid = [sb(f"gid{i}", [P, 1], I32) for i in range(XD)]
        aid = [sb(f"aid{i}", [P, 1], I32) for i in range(XD)]
        xg = [sb(f"xg{i}", [P, XR]) for i in range(XD)]
        ew_h = [sb(f"ew{i}_h", [P, 3, D], F16) for i in range(XD)]
        ew_l = [sb(f"ew{i}_l", [P, 3, D], F16) for i in range(XD)]
        ew = [sb(f"ew{i}", [P, 3, D]) for i in range(2)]
        eg_h = [sb(f"eg{i}_h", [P, C2, P], F16) for i in range(2)]
        eg_l = [sb(f"eg{i}_l", [P, C2, P], F16) for i in range(2)]
        eth = [sb(f"eth{i}", [P, P]) for i in range(2)]
        ega = [sb(f"ega{i}", [P, P]) for i in range(2)]
        eac = [sb(f"eac{i}", [P, P]) for i in range(2)]
        ea_h = [sb(f"ea{i}_h", [P, P], F16) for i in range(2)]
        ea_l = [sb(f"ea{i}_l", [P, P], F16) for i in range(2)]
        ewt = [sb(f"ewt{i}", [P, 1]) for i in range(XD)]
        ey = [sb(f"ey{i}", [P, D]) for i in range(2)]

        consts = sem("consts")
        consts2 = sem("consts2")
        setup_dma = sem("setup_dma")
        small_dma = sem("small_dma")
        gates_tanh = sem("gates_tanh")
        setup_hi = sem("setup_hi")
        setup_lo = sem("setup_lo")
        setup_dve = sem("setup_dve")
        table_dma = sem("table_dma")
        x_in, ctx_in = sem("x_in"), sem("ctx_in")
        ln_st, ln_pool = sem("ln_st"), sem("ln_pool")
        ln_cf, ln_nm, ln_dve = sems("ln_cf", 3), sems("ln_nm", 4), sems("ln_dve", 3)
        tr_rdy, tr_hi, tr_lo = (sems(n, 5) for n in ("tr_rdy", "tr_hi", "tr_lo"))
        ctx_split, kv_rdy, v_rdy = sem("ctx_split"), sem("kv_rdy"), sem("v_rdy")
        x1_copied = sem("x1_copied")
        kp_ev, v_ev, vr_ev, vp_ev = sem("kp_ev"), sem("v_ev"), sem("vr_ev"), sem("vp_ev")
        q_rdy, q_ev, s_rdy, s_ev, l_ok = sem("q_rdy"), sem("q_ev"), sem("s_rdy"), sem("s_ev"), sem("l_ok")
        sv_rdy, sv_ev, x1_ok = sem("sv_rdy"), sem("sv_ev"), sem("x1_ok")
        l0_rdy, l0_hi, l0_lo = (many(n, FK // 2) for n in ("l0_rdy", "l0_hi", "l0_lo"))
        l1_rdy, l1_hi, l1_lo = (many(n, FK // 2) for n in ("l1_rdy", "l1_hi", "l1_lo"))
        l2_rdy, x2_ok = sem("l2_rdy"), sem("x2_ok")
        pad_ok, lt_ok, sg_ok = sem("pad_ok"), sem("lt_ok"), sem("sg_ok")
        cx_ok, kr_hi = sem("cx_ok"), sem("kr_hi")
        handoff, kb_ok, ctx_hi = sem("handoff"), sem("kb_ok"), sem("ctx_hi")
        qp_rdy, qp_hi, qp_lo = sem("qp_rdy"), sem("qp_hi"), sem("qp_lo")
        am_rdy, hot_ok, c_dve = sem("am_rdy"), sem("hot_ok"), sem("c_dve")
        cnt_rdy, mrow_ok, vc_ok = sem("cnt_rdy"), sem("mrow_ok"), sem("vc_ok")
        lg_rdy, z_ok, p_ok = (many(n, 4) for n in ("lg_rdy", "z_ok", "p_ok"))
        pt_rdy, pt_hi_ok, pt_lo_ok = (many(n, 8) for n in ("pt_rdy", "pt_hi_ok", "pt_lo_ok"))
        av_rdy, av_ev = many("av_rdy", 4), many("av_ev", 4)
        av_dve, mx_dve = sem("av_dve"), sem("mx_dve")
        wc_rdy, x3_ok = sem("wc_rdy"), sem("x3_ok")
        rt_rdy, rt_max, rt_exp, rt_dve, ch_ok = (sem(n) for n in ("rt_rdy", "rt_max", "rt_exp", "rt_dve", "ch_ok"))
        cp_rdy, pos_ev, slots_ok, scattered, xr_out = (sem(n) for n in ("cp_rdy", "pos_ev", "slots_ok", "scattered", "xr_out"))
        gu_rdy, gu_th, gu_ac, gu_dve = many("gu_rdy", 4), many("gu_th", 4), many("gu_ac", 4), sem("gu_dve")
        ac_hi, ac_lo = many("ac_hi", 4), many("ac_lo", 4)
        dn_rdy, x4_ok, x4_out, tok_ok = sem("dn_rdy"), sem("x4_ok"), sem("x4_out"), sem("tok_ok")

        e_x, e_w = sems("e_x", XD), sems("e_w", 2)
        ids_in, ids_f, ids_t, ids_ok, e_gid, e_aid, e_out = (
            sem(n) for n in ("ids_in", "ids_f", "ids_t", "ids_ok", "e_gid", "e_aid", "e_out"))
        e_wh, e_wl, e_tr, e_trh, e_trl, e_gu, e_th, e_ga = (
            sem(n) for n in ("e_wh", "e_wl", "e_tr", "e_trh", "e_trl", "e_gu", "e_th", "e_ga"))
        e_ac, e_ach, e_acl, e_dn, e_wt, e_y = (sem(n) for n in ("e_ac", "e_ach", "e_acl", "e_dn", "e_wt", "e_y"))

        def each_expert(eng, step):
            for e in range(XD):
                step(e, e)
            with eng.Fori(1, E // XD - 1) as i:
                for u in range(XD):
                    step(i * XD + u, u)
            for e in range(E - XD, E):
                step(e, e % XD)

        def within(e, ahead):
            return not isinstance(e, int) or 0 <= e + ahead < E

        def fold(ap):
            return ap.rearrange("(c p) n -> p c n", p=P)

        splits = [
            (fold(wq0), wq_h[:, :, :], wq_l[:, :, :]),
            (fold(wk0), wk_h[:, :, :], wk_l[:, :, :]),
            (fold(wv0), wv_h[:, :, 0:D], wv_l[:, :, 0:D]),
            (fold(wkvT1[:, DH:2 * DH]), wv_h[:, :, D:VN], wv_l[:, :, D:VN]),
            (fold(wkvT1[:, 0:DH]), None, None),
            (fold(wqT1), wp_h[:, :, :], wp_l[:, :, :]),
            (fold(wcT1), wc_h[:, :, :], wc_l[:, :, :]),
            (fold(gates_w), gw_h[:, :, :], gw_l[:, :, :]),
            (fold(sgu_w), gu_h[:, :, :], gu_l[:, :, :]),
            (fold(sdown_w), dn_h[:, :, :], dn_l[:, :, :]),
        ]

        def staged(src):
            c, n = src.shape[1], src.shape[2]
            return stage[:, 0:c * n].rearrange("p (c n) -> p c n", c=c)

        bools = [(k0, 4, F), (k1, FK, F), (k2, FK, D)]
        nsplit = len(splits)

        block = es.enter_context(nc.Block())

        @block.sync
        def _(sp):
            small = [(raw[:, 0:2], g_xattn), (raw[:, 2:4], g_ffn), (raw[:, 4:5], s0), (raw[:, 5:6], s1),
                     (raw[:, 6:7], s2), (bv[:, :], bv0)]
            for dst, src in small:
                sp.dma_start(dst, src.partition_broadcast(P)).then_inc(small_dma, 16)
            sp.dma_start(bqk[:, 0, :], bq0).then_inc(small_dma, 16)
            sp.dma_start(bqk[:, 1, :], bk0).then_inc(small_dma, 16)
            sp.dma_start(mT[:, :], maskT).then_inc(small_dma, 16)
            sp.wait_ge(consts, 1)
            sp.dma_start(table.rearrange("(e c) o -> e (c o)", c=CAP), sent[:, :]).then_inc(table_dma, 16)
            sp.wait_ge(consts2, 26)
            sp.dma_start(out[NT:NT + CAP], xg[0][:, 0:D]).then_inc(table_dma, 16)
            for i, (src, _, _) in enumerate(splits):
                w(sp, setup_lo, i)
                sp.dma_start(staged(src), src).then_inc(setup_dma, 16)
            for i, (src, c, n) in enumerate(bools):
                w(sp, setup_lo, nsplit + i)
                sp.dma_start(stage32[:, 0:c * n // 4].rearrange("p (c n) -> p c n", c=c),
                             src.rearrange("(c p) n -> p c n", p=P)).then_inc(setup_dma, 16)

            def load_x(b):
                w(sp, x1_ok, b)
                sp.dma_start(x0[:, :, :], x[bass.ds(b, 1)].rearrange("o (t p) d -> p (o t) d", p=P)).then_inc(x_in, 16)

            def load_ctx(b):
                w(sp, ctx_split, b)
                sp.dma_start(ctx[:, :, :], ctxT[bass.ds(b, 1)].rearrange("o (c p) k -> p (o c) k", p=P)).then_inc(ctx_in, 16)

            def store_rows(b):
                sp.wait_ge(ch_ok, b + 1)
                sp.wait_ge(ln_nm[3], b + 1)
                sp.dma_start(xrows[bass.ds(b * S, S)].rearrange("(t p) n -> p t n", p=P), xr[:, :, :]).then_inc(xr_out, 16)

            def store_x4(b):
                sp.wait_ge(x4_ok, b + 1)
                sp.dma_start(out[bass.ds(b * S, S)].rearrange("(t p) n -> p t n", p=P), x4[:, :, :]).then_inc(x4_out, 16)

            load_x(0)
            load_ctx(0)
            load_x(1)
            load_ctx(1)
            load_x(2)
            load_ctx(2)
            load_x(3)
            store_x4(0)
            load_ctx(3)
            store_rows(0)
            load_x(4)
            store_x4(1)
            with sp.Fori(3, NB - 2) as n:
                load_ctx(n + 1)
                store_rows(n - 2)
                load_x(n + 2)
                store_x4(n - 1)
            load_ctx(NB - 1)
            store_rows(NB - 4)
            store_x4(NB - 3)
            store_rows(NB - 3)
            store_x4(NB - 2)
            store_rows(NB - 2)
            store_x4(NB - 1)
            store_rows(NB - 1)
            sp.wait_ge(scattered, 16 * T2 * TOPK * NB)

            sp.dma_start(slots_row[:, :], table.rearrange("(e c) o -> e (c o)", c=CAP)).then_inc(ids_in, 16)

            def load_weights(e, u):
                w(sp, e_wl, e - 1)
                sp.dma_start(ew[u % 2][:, 0:2, :], egu_w[bass.ds(e, 1)].rearrange("o (c p) n -> p (o c) n", p=P)).then_inc(e_w[u % 2], 16)
                sp.dma_start(ew[u % 2][:, 2, :], edown_w[bass.ds(e, 1)].rearrange("o p n -> p (o n)")).then_inc(e_w[u % 2], 16)

            each_expert(sp, load_weights)
            sp.wait_ge(e_out, 16 * E)

        @block.gpsimd
        def _(pool):
            g = nc.gpsimd
            g.iota(sent[:, :], pattern=[[1, CAP]], base=NT, channel_multiplier=0).then_inc(consts, 1)
            g.memset(ident[:, :], 0.0).then_inc(consts2, 1)
            g.memset(before16[:, :], 1.0).then_inc(consts2, 1)
            g.memset(row0[:, :], 1.0).then_inc(consts2, 1)
            g.memset(headmask[:, :], 1.0).then_inc(consts2, 1)
            pool.wait_ge(consts2, 4)
            g.affine_select(out=ident[:, :], in_=ident[:, :], compare_op=ALU.not_equal, fill=1.0,
                            base=0, pattern=[[-1, P]], channel_multiplier=1).then_inc(consts2, 1)
            g.affine_select(out=before16[:, :], in_=before16[:, :], compare_op=ALU.is_gt, fill=0.0,
                            base=0, pattern=[[1, P]], channel_multiplier=-1).then_inc(consts2, 1)
            g.affine_select(out=row0[:, :], in_=row0[:, :], compare_op=ALU.is_equal, fill=0.0,
                            base=0, pattern=[[0, P]], channel_multiplier=1).then_inc(consts2, 1)
            g.affine_select(out=headmask[:, :], in_=headmask[:, :], compare_op=ALU.is_ge, fill=0.0,
                            base=0, pattern=[[-DH, HC]], channel_multiplier=1).then_inc(consts2, 1)
            pool.wait_ge(consts2, 8)
            g.affine_select(out=headmask[:, :], in_=headmask[:, :], compare_op=ALU.is_gt, fill=0.0,
                            base=DH, pattern=[[DH, HC]], channel_multiplier=-1).then_inc(consts2, 1)
            g.iota(iota_k[:, :], pattern=[[1, S2]], base=0, channel_multiplier=0,
                   allow_small_or_imprecise_dtypes=True).then_inc(consts2, 1)
            g.iota(ebase[:, :], pattern=[[-CAP, E]], base=NT, channel_multiplier=0,
                   allow_small_or_imprecise_dtypes=True).then_inc(consts2, 1)
            g.iota(tokf[:, :], pattern=[[P, T2]], base=-S, channel_multiplier=1,
                   allow_small_or_imprecise_dtypes=True).then_inc(consts2, 1)
            g.memset(ones16[:, :], 1.0).then_inc(consts2, 1)
            g.memset(epsc[:, :], EPS).then_inc(consts2, 1)
            g.memset(threehalf[:, :], 1.5).then_inc(consts2, 1)
            g.memset(carry[:, :], 0.0).then_inc(consts2, 1)
            g.memset(ctx_h[:, :, :], 0.0).then_inc(consts2, 1)
            g.memset(ctx_l[:, :, :], 0.0).then_inc(consts2, 1)
            for rows in xg:
                g.memset(rows[:, :], 0.0).then_inc(consts2, 1)
            g.memset(vc_h[:, :], 0.0).then_inc(consts2, 1)
            g.memset(vc_l[:, :], 0.0).then_inc(consts2, 1)
            g.memset(mv[1][:, :, :], 0.0).then_inc(consts2, 1)

            g.memset(pool_pad[:, :], 0.0).then_inc(consts2, 1)
            pool.wait_ge(consts2, 26)

            def plain(site):
                return g.tensor_tensor(pool_pad[:, site:site + 1], epsc[:, :], epsc[:, :], ALU.mult)

            def split_ctx(b):
                pool.wait_ge(ctx_in, 16 * b + 16)
                w(pool, v_rdy, b)
                w(pool, cx_ok, 2 * b)
                plain(0)
                g.tensor_copy(ctx_h[:, :, 0:S2], ctx[:, :, :]).then_inc(ctx_hi, 1)
                pool.wait_ge(ctx_hi, b + 1)
                g.tensor_tensor(ctx_l[:, :, 0:S2], ctx[:, :, :], ctx_h[:, :, 0:S2], ALU.subtract).then_inc(ctx_split, 1)

            def take_ctx(b):
                pool.wait_ge(ctx_split, b + 1)
                w(pool, am_rdy, b)
                plain(7)
                g.tensor_copy(cx_h[:, :, :], ctx_h[:, :, 0:S2]).then_inc(cx_ok, 1)
                g.tensor_copy(cx_l[:, :, :], ctx_l[:, :, 0:S2]).then_inc(cx_ok, 1)

            def take_keys(b):
                pool.wait_ge(kp_ev, b + 1)
                pool.wait_ge(vp_ev, b + 1)
                w(pool, lg_rdy.sem, lg_rdy.nth(3, b - 1))
                w(pool, vc_ok, b)
                plain(1)
                g.tensor_copy(vpc[:, :], vp32[:, :]).then_inc(kr_hi, 1)
                g.tensor_copy(kr_h[:, :], kr32[:, :]).then_inc(kr_hi, 1)
                pool.wait_ge(kr_hi, 2 * b + 2)
                g.tensor_tensor(kr_l[:, :], kr32[:, :], kr_h[:, :], ALU.subtract).then_inc(handoff, 1)
                hm = headmask[:, :].unsqueeze(2).to_broadcast([P, HC, S2])
                pool.wait_ge(handoff, b + 1)
                g.tensor_tensor(kb_h[:, :, :], kr_h[:, :].unsqueeze(1).to_broadcast([P, HC, S2]), hm, ALU.mult).then_inc(kb_ok, 1)
                g.tensor_tensor(kb_l[:, :, :], kr_l[:, :].unsqueeze(1).to_broadcast([P, HC, S2]), hm, ALU.mult).then_inc(kb_ok, 1)

            def scatter(b):
                pool.wait_ge(slots_ok, b + 1)
                pool.wait_ge(tok_ok, b + 1)
                if not isinstance(b, int):
                    plain(0)
                for t in range(T2):
                    for k in range(TOPK):
                        g.indirect_dma_start(
                            out=table, out_offset=bass.IndirectOffsetOnAxis(ap=slot[:, t, k:k + 1], axis=0),
                            in_=toki[:, t:t + 1], in_offset=None, bounds_check=NT - 1, oob_is_err=False,
                        ).then_inc(scattered, 16)

            def keep_x1(b):
                pool.wait_ge(x1_ok, b + 1)
                w(pool, x2_ok, b)
                if not isinstance(b, int):
                    plain(2)
                g.tensor_copy(x1_kept[:, :, :], x1[:, :, :]).then_inc(x1_copied, 1)

            norm_chain = Steps(pool, ln_pool, 13)

            def ln_norm(b):
                pool.wait_ge(ln_st, b + 1)
                w(pool, tr_rdy[0], b)
                ch = norm_chain
                ch.start(b)
                y, half, step = rs[0], nt[0][:, 0, :], nt[0][:, 1, :]
                for k in range(3):
                    if k:
                        ch.wait()
                    ch.did(g.tensor_tensor(step, y, y, ALU.mult))
                    ch.wait()
                    ch.did(g.tensor_tensor(step, step, half, ALU.mult))
                    ch.wait()
                    ch.did(g.tensor_tensor(step, step, threehalf[:, :], ALU.add))
                    ch.wait()
                    ch.did(g.tensor_tensor(y, step, y, ALU.mult))
                ch.wait()
                ch.did(g.tensor_tensor(nb[0], mv[0][:, :, 0], y, ALU.mult))
                ch.wait()
                plain(2)
                for t in range(T2):
                    last = g.tensor_scalar(xn[0][:, t, :], x0[:, t, :], y[:, t:t + 1], nb[0][:, t:t + 1], ALU.mult, ALU.subtract)
                last.then_inc(ln_nm[0], 1)
                ch.end()

            def rows(n, last=False):
                take_ctx(n)
                if not last:
                    split_ctx(n + 1)
                    ln_norm(n + 1)
                take_keys(n)

            pool.wait_ge(table_dma, 32)
            split_ctx(0)
            ln_norm(0)
            keep_x1(0)
            rows(0)
            keep_x1(1)
            rows(1)
            keep_x1(2)
            rows(2)
            scatter(0)
            keep_x1(3)
            with pool.Fori(3, NB - 1) as n:
                rows(n)
                scatter(n - 2)
                keep_x1(n + 1)
            rows(NB - 1, last=True)
            for b in range(NB - 3, NB):
                scatter(b)
            pool.wait_ge(xr_out, 16 * NB)
            pool.wait_ge(x4_out, 16 * NB)

            def gather(e, u):
                pool.wait_ge(e_gid, e + 1)
                w(pool, e_tr, e - XD + 1)
                w(pool, e_wt, e - XD + 1)
                if not isinstance(e, int):
                    plain(3).then_inc(pad_ok, 1)
                g.indirect_dma_start(
                    out=xg[u][:, :], out_offset=None, in_=xrows,
                    in_offset=bass.IndirectOffsetOnAxis(ap=gid[u][:, 0:1], axis=0),
                    bounds_check=NT - 1, oob_is_err=False).then_inc(e_x[u], 16)

            def add_out(e, u):
                pool.wait_ge(e_y, e + 1)
                pool.wait_ge(e_aid, e + 1)
                w(pool, e_out, 16 * e)
                if not isinstance(e, int):
                    plain(4).then_inc(pad_ok, 1)
                g.indirect_dma_start(
                    out=out, out_offset=bass.IndirectOffsetOnAxis(ap=aid[u][:, 0:1], axis=0),
                    in_=ey[u % 2][:, :], in_offset=None, bounds_check=NT + CAP - 1, oob_is_err=True,
                    compute_op=ALU.add).then_inc(e_out, 16)

            g.memset(pool_pad[:, 3:5], 0.0).then_inc(pad_ok, 2)
            for e in range(XD - 1):
                gather(e, e)

            def step(e, u):
                if not isinstance(e, int):
                    pool.wait_ge(pad_ok, 2 * (e - XD + 1))
                if within(e, XD - 1):
                    gather(e + XD - 1, (u - 1) % XD)
                if within(e, -1):
                    add_out(e - 1, (u - 1) % XD)

            each_expert(pool, step)
            add_out(E - 1, (E - 1) % XD)

        @block.scalar
        def _(act):
            a = nc.scalar
            act.wait_ge(small_dma, 16 * 9)
            a.activation(tg[:, :], raw[:, 0:4], ACT.Tanh).then_inc(gates_tanh, 1)
            for i, (src, hi, lo) in enumerate(splits):
                act.wait_ge(setup_dma, 16 * (i + 1))
                if hi is None:
                    for h in range(HC):
                        last = a.activation(wkr_h[:, :, h * DH:(h + 1) * DH], staged(src), ACT.Copy, scale=WS)
                    last.then_inc(setup_hi, 1)
                else:
                    a.activation(hi, staged(src), ACT.Copy, scale=WS).then_inc(setup_hi, 1)
            act.wait_ge(consts2, 26)

            def ln_norm(i, b, src, dst):
                act.wait_ge(ln_cf[(0, 1, 1, 2)[i]], b + (2 if i == 2 else 1))
                for t in range(T2):
                    ins = a.activation(dst[:, t, 0:D], src[:, t, :], ACT.Identity, bias=nb[i][:, t:t + 1], scale=rs[i][:, t:t + 1])
                ins.then_inc(ln_nm[i], 1)

            def tr_high(i, b, dst):
                act.wait_ge(tr_rdy[i], b + 1)
                a.activation(dst[:, :, :], two(ps_tr), ACT.Copy).then_inc(tr_hi[i], 1)

            def a_kv(b):
                act.wait_ge(kv_rdy, b + 1)
                w(act, s_rdy, b)
                w(act, handoff, b)
                for c in range(C2):
                    a.activation(kp32[:, c, :], ps_lg[:, 0, c * P:(c + 1) * P], ACT.Relu, bias=bqk[:, 1, c:c + 1], scale=1 / WS)
                a.activation(kr32[:, :], ps_lg[:, 0, 2 * P:2 * P + S2], ACT.Copy, scale=1 / WS).then_inc(kp_ev, 1)

            def a_vals(b):
                act.wait_ge(v_ev, b + 1)
                a.activation(vp32[:, :], ps_pt0[0:S2, D:VN], ACT.Copy, scale=1 / WS).then_inc(vp_ev, 1)
                w(act, sv_rdy, b)
                a.activation(v32r[:, :], v32[:, :], ACT.Relu).then_inc(vr_ev, 1)

            def a_q(b):
                act.wait_ge(q_rdy, b + 1)
                for c in range(C2):
                    ins = a.activation(q32[:, c, :], ps_lg[:, 1, c * S:(c + 1) * S], ACT.Relu, bias=bqk[:, 0, c:c + 1], scale=1 / WS)
                ins.then_inc(q_ev, 1)

            def a_s(b):
                act.wait_ge(s_rdy, b + 1)
                w(act, l_ok, b)
                a.activation(s32[:, :], ps_lg[0:S2, 0, 0:S], ACT.Relu, scale=1 / 16.0).then_inc(s_ev, 1)

            def a_sv(b):
                act.wait_ge(sv_rdy, b + 1)
                w(act, x1_ok, b)
                a.activation(o32[:, :, :], ps_lg[:, 1, :].rearrange("p (t n) -> p t n", t=T2), ACT.Relu).then_inc(sv_ev, 1)

            def b_l0(j, b):
                act.wait_ge(l0_rdy.sem, l0_rdy.nth(j, b))
                a.activation(h0_h[:, 2 * j:2 * j + 2, :], two(bank[j % 2]), ACT.Relu).then_inc(l0_hi.sem, 1)

            def b_l1(j, b):
                act.wait_ge(l1_rdy.sem, l1_rdy.nth(j, b))
                w(act, l2_rdy, b)
                a.activation(h1_h[:, 2 * j:2 * j + 2, :], two(bank[j % 2]), ACT.Relu).then_inc(l1_hi.sem, 1)

            def c_qp(b):
                act.wait_ge(qp_rdy, b + 1)
                a.activation(qp_h[:, :, :], two(ps_m), ACT.Copy, scale=1 / WS).then_inc(qp_hi, 1)

            def c_exp(r, b):
                act.wait_ge(z_ok.sem, z_ok.nth(r, b))
                if r:
                    act.wait_ge(pt_rdy.sem, pt_rdy.nth(2 * r - 1, b))
                else:
                    w(act, pt_rdy.sem, pt_rdy.nth(7, b - 1))
                a.activation(p32[:, :, :], z[:, :, :], ACT.Exp, scale=1 / float(np.sqrt(DH))).then_inc(p_ok.sem, 1)

            def c_pt(k, b):
                act.wait_ge(pt_rdy.sem, pt_rdy.nth(k, b))
                a.activation(pt_h[:, k % 2 * HB:(k % 2 + 1) * HB, :], ps_pt[k % 2][0:S2, :].rearrange("p (h n) -> p h n", h=HB),
                             ACT.Copy).then_inc(pt_hi_ok.sem, 1)

            def d_route(b):
                act.wait_ge(rt_max, b + 1)
                w(act, ch_ok, b)
                for t in range(T2):
                    a.activation(ex[:, t, :], ps_pt0[:, t * (E + 1):t * (E + 1) + E], ACT.Exp, bias=ltm[:, t:t + 1], scale=1 / WS)
                a.activation(sgt[:, :], ps_pt0[:, 0:T2 * (E + 1)].rearrange("p (t n) -> p t n", t=T2)[:, :, E],
                             ACT.Tanh, scale=0.5 / WS).then_inc(rt_exp, 1)

            def d_gu(j, b):
                act.wait_ge(gu_rdy.sem, gu_rdy.nth(j, b))
                w(act, gu_ac.sem, gu_ac.nth(j, b - 1))
                a.activation(th[:, j, :], bank[j % 2][:, 0:S], ACT.Tanh, scale=0.5 / WS).then_inc(gu_th.sem, 1)

            def d_ac(j, b):
                act.wait_ge(gu_ac.sem, gu_ac.nth(j, b))
                w(act, dn_rdy, b)
                a.activation(ac_h[:, j, :], ac[:, j, :], ACT.Copy).then_inc(ac_hi.sem, 1)

            def first(n, c, m, d):
                if n is not None:
                    w(act, l1_rdy.sem, l1_rdy.nth(3, n - 1))
                    for j in range(4):
                        b_l0(j, n)
                    b_l1(0, n)
                if c is not None:
                    c_exp(0, c)
                if n is not None:
                    b_l1(1, n)
                for r in range(4):
                    if c is not None:
                        c_pt(2 * r, c)
                        c_pt(2 * r + 1, c)
                        if r < 3:
                            c_exp(r + 1, c)
                    if n is not None and r == 1:
                        b_l1(2, n)
                    if m is not None and r == 1:
                        tr_high(0, m, xt_h[0])
                if n is not None:
                    b_l1(3, n)

            def second(n, c, m, d):
                if m is not None:
                    a_q(m)
                if c is not None:
                    tr_high(4, c, at_h)
                if m is not None:
                    a_kv(m)
                    a_vals(m)
                    a_s(m)
                    a_sv(m)
                if c is not None:
                    w(act, xr_out, 16 * c)
                    ln_norm(3, c, x3, xr)
                    tr_high(3, c, xt_h[3])
                    d_route(c)
                    d_gu(0, c)
                    d_gu(1, c)
                    d_ac(0, c)
                if m is not None:
                    ln_norm(1, m, x1, xn[1])
                    tr_high(1, m, xt_h[1])
                if n is not None:
                    ln_norm(2, n, x2, xn[2])
                if c is not None:
                    d_ac(1, c)
                    d_gu(2, c)
                if n is not None:
                    tr_high(2, n, xt_h[2])
                if c is not None:
                    d_gu(3, c)
                    d_ac(2, c)
                    d_ac(3, c)
                if n is not None:
                    c_qp(n)

            first(None, None, 0, None)
            second(None, None, 0, None)
            first(0, None, 1, None)
            second(0, None, 1, None)
            first(1, 0, 2, None)
            second(1, 0, 2, None)
            first(2, 1, 3, 0)
            second(2, 1, 3, 0)
            with act.Fori(3, NB - 1) as n:
                first(n, n - 1, n + 1, n - 2)
                second(n, n - 1, n + 1, n - 2)
            first(NB - 1, NB - 2, None, NB - 3)
            second(NB - 1, NB - 2, None, NB - 3)
            first(None, NB - 1, None, NB - 2)
            second(None, NB - 1, None, NB - 2)
            first(None, None, None, NB - 1)

            def split_weights(e, u):
                act.wait_ge(e_w[u % 2], (e - u % 2) * 16 + 32)
                w(act, e_dn, e - XD + 1)
                a.activation(ew_h[u][:, :, :], ew[u % 2][:, :, :], ACT.Copy, scale=WS).then_inc(e_wh, 1)

            def rows_high(e, u):
                act.wait_ge(e_tr, e + 1)
                w(act, e_gu, e - 1)
                a.activation(eg_h[u % 2][:, :, :], ps_eg[u % 2][:, 0:D].rearrange("p (c n) -> p c n", c=C2), ACT.Copy).then_inc(e_trh, 1)

            def expert(e, u):
                if within(e, 1):
                    rows_high(e + 1, (u + 1) % XD)
                act.wait_ge(e_gu, e + 1)
                w(act, e_ga, e - 1)
                a.activation(eth[u % 2][:, :], bank[u % 2][:, 0:P], ACT.Tanh, scale=0.5 / WS).then_inc(e_th, 1)
                act.wait_ge(e_ac, e + 1)
                w(act, e_dn, e - 1)
                a.activation(ea_h[u % 2][:, :], eac[u % 2][:, :], ACT.Copy).then_inc(e_ach, 1)
                if within(e, 2):
                    split_weights(e + 2, (u + 2) % XD)

            split_weights(0, 0)
            split_weights(1, 1)
            rows_high(0, 0)
            each_expert(act, expert)

        @block.tensor
        def _(pe):
            mm = nc.tensor.matmul

            def three(out_, parts, start=True, stop=True):
                seq = [(sh, mh) for sh, sl, mh, ml in parts] + [(sh, ml) for sh, sl, mh, ml in parts] \
                    + [(sl, mh) for sh, sl, mh, ml in parts]
                for i, (s_, m_) in enumerate(seq):
                    ins = mm(out_, s_, m_, start=(start and i == 0), stop=(stop and i == len(seq) - 1))
                return ins

            def transposes(i, b, src):
                pe.wait_ge(ln_nm[i], b + 1)
                for t in range(T2):
                    for c in range(C2):
                        ins = nc.tensor.transpose(two(ps_tr)[:, c, t * P:(t + 1) * P], src[:, t, c * P:(c + 1) * P], ident[:, :])
                ins.then_inc(tr_rdy[i], 1)

            def a_kv(b):
                pe.wait_ge(ctx_split, b + 1)
                for m in range(C2):
                    three(ps_lg[:, 0, m * P:(m + 1) * P],
                          [(wk_h[:, c, m * P:(m + 1) * P], wk_l[:, c, m * P:(m + 1) * P], ctx_h[:, c, :], ctx_l[:, c, :]) for c in range(C2)])
                three(ps_lg[:, 0, 2 * P:3 * P],
                      [(wkr_h[:, c, :], wkr_l[:, c, :], ctx_h[:, c, :], ctx_l[:, c, :]) for c in range(C2)]).then_inc(kv_rdy, 1)

            def a_vals(b):
                three(ps_pt0[:, 0:VN],
                      [(ctx_h[:, c, :], ctx_l[:, c, :], wv_h[:, c, :], wv_l[:, c, :]) for c in range(C2)]).then_inc(v_rdy, 1)

            def feature_major(dst, wh, wl, xh, xl):
                for m in range(C2):
                    ins = three(dst[:, m, :],
                                [(wh[:, c, m * P:(m + 1) * P], wl[:, c, m * P:(m + 1) * P], xh[:, c, :], xl[:, c, :]) for c in range(C2)])
                return ins

            def a_q(b):
                pe.wait_ge(tr_lo[0], b + 1)
                feature_major(ps_lg[:, 1, :].rearrange("p (a n) -> p a n", a=2), wq_h, wq_l, xt_h[0], xt_l[0]).then_inc(q_rdy, 1)

            def a_s(b):
                pe.wait_ge(kp_ev, b + 1)
                pe.wait_ge(q_ev, b + 1)
                for c in range(C2):
                    ins = mm(ps_lg[:, 0, 0:S], kp32[:, c, :], q32[:, c, :], start=(c == 0), stop=(c == C2 - 1))
                ins.then_inc(s_rdy, 1)

            def a_sv(b):
                pe.wait_ge(l_ok, b + 1)
                pe.wait_ge(vr_ev, b + 1)
                for t in range(T2):
                    ins = mm(ps_lg[:, 1, t * D:(t + 1) * D], l32[:, t * P:(t + 1) * P], v32r[:, :], start=True, stop=True)
                ins.then_inc(sv_rdy, 1)

            def b_l0(j, b):
                if j == 0:
                    pe.wait_ge(tr_lo[1], b + 1)
                    w(pe, gu_ac.sem, gu_ac.nth(2, b - 2))
                elif j == 1:
                    w(pe, gu_ac.sem, gu_ac.nth(3, b - 2))
                else:
                    pe.wait_ge(l0_lo.sem, l0_lo.nth(j - 2, b))
                for m in (2 * j, 2 * j + 1):
                    for k, (s_, m_) in enumerate([(wb0[:, c, m * P:(m + 1) * P], xp[:, c, :]) for xp in (xt_h[1], xt_l[1]) for c in range(C2)]):
                        ins = mm(two(bank[j % 2])[:, m % 2, :], s_, m_, start=(k == 0), stop=(k == 3))
                ins.then_inc(l0_rdy.sem, 1)

            def b_l1(m, b):
                j = m // 2
                if m % 2 == 0:
                    if j < 2:
                        pe.wait_ge(l0_lo.sem, l0_lo.nth(j + 2, b))
                        pe.wait_ge(l0_lo.sem, l0_lo.nth(3, b))
                    else:
                        pe.wait_ge(l1_lo.sem, l1_lo.nth(j - 2, b))
                for i, hp in enumerate((h0_h, h0_l)):
                    for k in range(FK):
                        ins = mm(two(bank[j % 2])[:, m % 2, :], wb1[:, k, m * P:(m + 1) * P], hp[:, k, :],
                                 start=(i == 0 and k == 0), stop=(i == 1 and k == FK - 1))
                if m % 2:
                    ins.then_inc(l1_rdy.sem, 1)

            def b_l2(t, b):
                if t == 0:
                    pe.wait_ge(l1_lo.sem, l1_lo.nth(3, b))
                    w(pe, pt_lo_ok.sem, pt_lo_ok.nth(7, b - 1))
                for i, hp in enumerate((h1_h, h1_l)):
                    for k in range(FK):
                        ins = mm(two(ps_yo)[:, t, :], hp[:, k, t * P:(t + 1) * P], wb2[:, k, :],
                                 start=(i == 0 and k == 0), stop=(i == 1 and k == FK - 1))
                if t == T2 - 1:
                    ins.then_inc(l2_rdy, 1)

            def c_qp(b):
                pe.wait_ge(tr_lo[2], b + 1)
                feature_major(two(ps_m), wp_h, wp_l, xt_h[2], xt_l[2]).then_inc(qp_rdy, 1)

            def c_am(b):
                pe.wait_ge(qp_lo, b + 1)
                pe.wait_ge(cx_ok, 2 * b + 2)
                for t in range(T2):
                    tt = slice(t * P, (t + 1) * P)
                    ins = three(ps_tr[:, t * S2:(t + 1) * S2],
                                [(qp_h[:, c, tt], qp_l[:, c, tt], cx_h[:, c, :], cx_l[:, c, :]) for c in range(C2)])
                ins.then_inc(am_rdy, 1)

            def c_cnt(b):
                pe.wait_ge(hot_ok, b + 1)
                for t in range(T2):
                    mm(ps_tr[:, 2 * P:2 * P + S2], ones16[:, :], hot[:, t, :], start=(t == 0), stop=(t == T2 - 1))
                for t in range(T2):
                    ins = mm(ps_tr[0:S2, 3 * P:3 * P + 1], hot[:, t, :], ones16[:, 0:1], start=(t == 0), stop=(t == T2 - 1))
                ins.then_inc(cnt_rdy, 1)

            def c_lg(r, b):
                t, c = divmod(r, C2)
                if r == 0:
                    pe.wait_ge(kb_ok, 2 * b + 2)
                    pe.wait_ge(mrow_ok, b + 1)
                else:
                    pe.wait_ge(z_ok.sem, z_ok.nth(r - 1, b))
                tt = slice(t * P, (t + 1) * P)
                for g_ in range(2):
                    dst = ps_lg[:, g_, 0:HB * S2]
                    hh = slice(g_ * HB, (g_ + 1) * HB)
                    mm(dst, row0[:, :], mrow[:, :, :], start=True, stop=False)
                    ins = three(dst, [(qp_h[:, c, tt], qp_l[:, c, tt], kb_h[:, hh, :], kb_l[:, hh, :])], start=False)
                ins.then_inc(lg_rdy.sem, 1)

            def c_pt(k, b):
                if k % 2 == 0:
                    pe.wait_ge(p_ok.sem, p_ok.nth(k // 2, b))
                if k >= 2:
                    pe.wait_ge(pt_lo_ok.sem, pt_lo_ok.nth(k - 2, b))
                elif k == 0:
                    w(pe, rt_exp, b)
                else:
                    w(pe, x4_ok, b)
                for h in range(HB):
                    ins = nc.tensor.transpose(ps_pt[k % 2][0:S2, h * P:(h + 1) * P], p32[:, k % 2 * HB + h, :], ident[:, :])
                ins.then_inc(pt_rdy.sem, 1)

            def c_av(r, b):
                pe.wait_ge(pt_lo_ok.sem, pt_lo_ok.nth(2 * r, b))
                pe.wait_ge(pt_lo_ok.sem, pt_lo_ok.nth(2 * r + 1, b))
                if r == 0:
                    pe.wait_ge(vc_ok, b + 1)
                else:
                    pe.wait_ge(av_ev.sem, av_ev.nth(r - 1, b))
                for h in range(HC):
                    ins = three(ps_m[:, h * VW:(h + 1) * VW], [(pt_h[:, h, :], pt_l[:, h, :], vc_h[:, :], vc_l[:, :])])
                ins.then_inc(av_rdy.sem, 1)

            def c_att(b):
                pe.wait_ge(av_ev.sem, av_ev.nth(3, b))
                for t in range(T2):
                    for c in range(C2):
                        ins = nc.tensor.transpose(two(ps_tr)[:, c, t * P:(t + 1) * P], att[:, t, c * P:(c + 1) * P], ident[:, :])
                ins.then_inc(tr_rdy[4], 1)

            def token_major(dst, xh, xl, wh, wl, kk):
                for t in range(T2):
                    tt = slice(t * P, (t + 1) * P)
                    ins = three(dst[:, t, :], [(xh[:, c, tt], xl[:, c, tt], wh[:, c, :], wl[:, c, :]) for c in range(kk)])
                return ins

            def c_wc(b):
                pe.wait_ge(tr_lo[4], b + 1)
                token_major(two(ps_m), at_h, at_l, wc_h, wc_l, C2).then_inc(wc_rdy, 1)

            def d_route(b):
                pe.wait_ge(tr_lo[3], b + 1)
                pe.wait_ge(pt_lo_ok.sem, pt_lo_ok.nth(6, b))
                token_major(ps_pt0[:, 0:T2 * (E + 1)].rearrange("p (t n) -> p t n", t=T2),
                            xt_h[3], xt_l[3], gw_h, gw_l, C2).then_inc(rt_rdy, 1)

            def d_gu(j, b):
                if j < 2:
                    w(pe, l1_lo.sem, l1_lo.nth(2 + j, b + 1 if not isinstance(b, int) else min(b + 1, NB - 1)))
                else:
                    pe.wait_ge(gu_ac.sem, gu_ac.nth(j - 2, b))
                for i in range(2):
                    m = i * SK + j
                    ins = three(two(bank[j % 2])[:, i, :],
                                [(gu_h[:, c, m * P:(m + 1) * P], gu_l[:, c, m * P:(m + 1) * P], xt_h[3][:, c, :], xt_l[3][:, c, :]) for c in range(C2)])
                ins.then_inc(gu_rdy.sem, 1)

            def d_cp(b):
                pe.wait_ge(ch_ok, b + 1)
                for t in range(T2):
                    dst = ps_tr[:, t * E:(t + 1) * E]
                    mm(dst, before16[:, :], chosen[:, t, :], start=True, stop=(t == 0))
                    if t:
                        mm(dst, ones16[:, :], chosen[:, 0, :], start=False, stop=True)
                for t in range(T2):
                    ins = mm(ps_tr[:, T2 * E:(T2 + 1) * E], ones16[:, :], chosen[:, t, :], start=(t == 0), stop=(t == T2 - 1))
                ins.then_inc(cp_rdy, 1)

            def d_dn(b):
                w(pe, x2_ok, b + 2 if not isinstance(b, int) else min(b + 2, NB))
                for t in range(T2):
                    tt = slice(t * P, (t + 1) * P)
                    for k in range(SK):
                        pe.wait_ge(ac_lo.sem, ac_lo.nth(k, b))
                        ins = three(two(ps_yo)[:, t, :], [(ac_h[:, k, tt], ac_l[:, k, tt], dn_h[:, k, :], dn_l[:, k, :])],
                                    start=(k == 0), stop=(k == SK - 1))
                ins.then_inc(dn_rdy, 1)

            def first(n, c, m, d):
                if n is not None:
                    for j in range(4):
                        b_l0(j, n)
                if c is not None:
                    c_am(c)
                if n is not None:
                    b_l1(0, n)
                    b_l1(1, n)
                if c is not None:
                    c_cnt(c)
                if n is not None:
                    b_l1(2, n)
                if c is not None:
                    if n is not None:
                        pe.wait_ge(x1_ok, n + 1)
                    c_lg(0, c)
                if n is not None:
                    b_l1(3, n)
                for r in range(4):
                    if c is not None:
                        c_pt(2 * r, c)
                        c_pt(2 * r + 1, c)
                        if r < 3:
                            c_lg(r + 1, c)
                    if m is not None and r == 1:
                        if c is not None:
                            pe.wait_ge(vc_ok, c + 1)
                        elif n is not None:
                            pe.wait_ge(tr_lo[1], n + 1)
                        transposes(0, m, xn[0])
                    if d is not None and r == 2:
                        if m is not None:
                            pe.wait_ge(tr_lo[0], m + 1)
                        elif c is not None:
                            pe.wait_ge(vc_ok, c + 1)
                        d_cp(d)
                    if n is not None:
                        b_l1(4 + r, n)
                    if c is not None:
                        c_av(r, c)

            def second(n, c, m, d):
                if m is not None:
                    if c is not None:
                        pe.wait_ge(z_ok.sem, z_ok.nth(3, c))
                        pe.wait_ge(pt_lo_ok.sem, pt_lo_ok.nth(6, c))
                    a_q(m)
                if c is not None:
                    if d is not None:
                        pe.wait_ge(pos_ev, d + 1)
                    c_att(c)
                if m is not None:
                    a_kv(m)
                    a_vals(m)
                if c is not None:
                    c_wc(c)
                if m is not None:
                    a_s(m)
                if n is not None:
                    b_l2(0, n)
                if m is not None:
                    a_sv(m)
                if n is not None:
                    b_l2(1, n)
                if c is not None:
                    pe.wait_ge(tr_lo[4], c + 1)
                    transposes(3, c, xr)
                    if m is not None:
                        pe.wait_ge(vp_ev, m + 1)
                    d_route(c)
                    d_gu(0, c)
                    d_gu(1, c)
                    d_gu(2, c)
                if m is not None:
                    if c is not None:
                        pe.wait_ge(tr_lo[3], c + 1)
                    else:
                        pe.wait_ge(tr_lo[0], m + 1)
                    transposes(1, m, xn[1])
                if c is not None:
                    d_gu(3, c)
                if n is not None:
                    if m is not None:
                        pe.wait_ge(tr_lo[1], m + 1)
                    else:
                        pe.wait_ge(tr_lo[3], c + 1)
                    transposes(2, n, xn[2])
                    c_qp(n)
                if c is not None:
                    d_dn(c)

            pe.wait_ge(consts2, 26)
            pe.wait_ge(setup_lo, nsplit + 3)
            first(None, None, 0, None)
            second(None, None, 0, None)
            first(0, None, 1, None)
            second(0, None, 1, None)
            first(1, 0, 2, None)
            second(1, 0, 2, None)
            first(2, 1, 3, 0)
            second(2, 1, 3, 0)
            with pe.Fori(3, NB - 1) as n:
                first(n, n - 1, n + 1, n - 2)
                second(n, n - 1, n + 1, n - 2)
            first(NB - 1, NB - 2, None, NB - 3)
            second(NB - 1, NB - 2, None, NB - 3)
            first(None, NB - 1, None, NB - 2)
            second(None, NB - 1, None, NB - 2)
            first(None, None, None, NB - 1)

            pe.wait_ge(x4_ok, NB)
            pe.wait_ge(tr_lo[3], NB)
            pe.wait_ge(pos_ev, NB)
            pe.wait_ge(gu_ac.sem, gu_ac.nth(3, NB - 1))
            pe.wait_ge(ids_f, 1)
            nc.tensor.transpose(ps_yo[:, 0:E], slots_f[:, :], ident[0:E, 0:E]).then_inc(ids_t, 1)

            def rows_turned(e, u):
                pe.wait_ge(e_x[u], (e - u) * (16 // XD) + 16)
                w(pe, e_trl, e - 1)
                for c in range(C2):
                    ins = nc.tensor.transpose(ps_eg[u % 2][:, c * P:(c + 1) * P], xg[u][:, c * P:(c + 1) * P], ident[:, :])
                ins.then_inc(e_tr, 1)

            def down(e, u):
                pe.wait_ge(e_acl, e + 1)
                w(pe, e_y, e - 1)
                three(ps_lg[:, u % 2, 0:D], [(ea_h[u % 2][:, :], ea_l[u % 2][:, :], ew_h[u][:, 2, :], ew_l[u][:, 2, :])]).then_inc(e_dn, 1)

            def expert(e, u):
                if within(e, 1):
                    rows_turned(e + 1, (u + 1) % XD)
                pe.wait_ge(e_trl, e + 1)
                pe.wait_ge(e_wl, e + 1)
                w(pe, e_ac, e - 1)
                for g_ in range(2):
                    cc = slice(g_ * IE, (g_ + 1) * IE)
                    ins = three(bank[u % 2][:, g_ * P:(g_ + 1) * P],
                                [(ew_h[u][:, c, cc], ew_l[u][:, c, cc], eg_h[u % 2][:, c, :], eg_l[u % 2][:, c, :]) for c in range(C2)])
                ins.then_inc(e_gu, 1)
                if within(e, -1):
                    down(e - 1, (u - 1) % XD)

            rows_turned(0, 0)
            each_expert(pe, expert)
            down(E - 1, (E - 1) % XD)

        @block.vector
        def _(dve):
            v = nc.vector
            ln_chain = [Steps(dve, ln_dve[g], 10 if g else 3) for g in range(3)]

            def plain(site):
                v.memset(dve_pad[:, site:site + 1], 0.0)

            cch = Steps(dve, c_dve, 5)
            rch = Steps(dve, rt_dve, 11)

            dve.wait_ge(small_dma, 16 * 9)
            dve.wait_ge(gates_tanh, 1)
            setup = Steps(dve, setup_dve, 14)
            setup.start(0)

            def do(ins):
                setup.did(ins)

            do(v.tensor_scalar(sg[:, :], raw[:, 4:6], 0.0, None, ALU.is_gt))
            do(v.tensor_scalar(ab[:, :], raw[:, 4:6], 0.0, None, ALU.is_lt))
            setup.wait()
            do(v.tensor_tensor(sg[:, :], sg[:, :], ab[:, :], ALU.subtract))
            setup.wait()
            do(v.tensor_tensor(ab[:, :], raw[:, 4:6], sg[:, :], ALU.mult))
            setup.wait()
            do(v.tensor_tensor(sc[:, 4:5], ab[:, 0:1], ab[:, 1:2], ALU.mult))
            do(v.tensor_tensor(sc[:, 5:6], tg[:, 2:3], raw[:, 6:7], ALU.mult))
            setup.wait()
            do(v.scalar_tensor_tensor(F0, sc[:, 4:5], 8.0 / HS, sc[:, 5:6], ALU.mult, ALU.mult))
            do(v.tensor_copy(G0X, tg[:, 0:1]))
            do(v.tensor_scalar(G1X, tg[:, 1:2], 1 / WS, None, ALU.mult))
            do(v.tensor_scalar(G1F, tg[:, 3:4], 0.5 / WS, None, ALU.mult))
            do(v.tensor_scalar(sc[:, 6:7], sg[:, 1:2], 2.0 * HS, None, ALU.mult))
            do(v.tensor_scalar(sc[:, 7:8], tg[:, 3:4], 1 / WS, None, ALU.mult))
            setup.wait()
            for i, (src, hi, lo) in enumerate(splits):
                dve.wait_ge(setup_hi, i + 1)
                if hi is None:
                    for h in range(HC):
                        hs = slice(h * DH, (h + 1) * DH)
                        last = v.scalar_tensor_tensor(wkr_l[:, :, hs], staged(src), WS, wkr_h[:, :, hs], ALU.mult, ALU.subtract)
                    last.then_inc(setup_lo, 1)
                else:
                    v.scalar_tensor_tensor(lo, staged(src), WS, hi, ALU.mult, ALU.subtract).then_inc(setup_lo, 1)
            dve.wait_ge(setup_dma, 16 * (nsplit + 1))
            s8 = stage8[:, 0:4 * F].rearrange("p (c n) -> p c n", c=4)
            do(v.tensor_tensor(wb0[:, :, :], s8[:, 0:C2, :], s8[:, C2:4, :], ALU.subtract))
            setup.wait()
            do(v.tensor_scalar(wb0[:, :, :], wb0[:, :, :], sg[:, 0:1], None, ALU.mult))
            setup.wait()
            dve.sem_inc(setup_lo, 1)
            dve.wait_ge(setup_dma, 16 * (nsplit + 2))
            v.tensor_scalar(wb1[:, :, :], stage8[:, 0:FK * F].rearrange("p (c n) -> p c n", c=FK),
                            0.5, sc[:, 6:7], ALU.subtract, ALU.mult).then_inc(setup_lo, 1)
            dve.wait_ge(setup_dma, 16 * (nsplit + 3))
            v.tensor_scalar(wb2[:, :, :], stage8[:, 0:FK * D].rearrange("p (c n) -> p c n", c=FK),
                            2.0, 1.0, ALU.mult, ALU.subtract).then_inc(setup_lo, 1)
            setup.end()
            dve.wait_ge(consts2, 26)

            def ln_stats(g, k, *srcs):
                ch = ln_chain[g]
                ch.start(k)
                for place, src, made, used in srcs:
                    w(dve, *used)
                    dve.wait_ge(*made)
                    for t in range(T2):
                        last = v.bn_stats(stats[g][:, place * T2 + t, :], src[:, t, :])
                ch.did(last)
                ch.wait()
                plain(8 + g)
                for place, *_ in srcs:
                    for t in range(T2):
                        last = v.bn_aggr(mv[g][:, place * T2 + t, :], stats[g][:, place * T2 + t, :])
                ch.did(last)
                ln_guess(g)

            def ln_guess(g):
                ch = ln_chain[g]
                half = nt[g][:, 0, :]
                ch.wait()
                ch.did(v.tensor_scalar(half, mv[g][:, :, 1], EPS, -0.5, ALU.add, ALU.mult))
                ch.wait()
                last = v.tensor_scalar(rs_g[g][:, :].bitcast(I32), half.bitcast(I32), -0.5, GUESS, ALU.mult, ALU.add)
                if g:
                    ch.did(last)
                else:
                    last.then_inc(ln_st, 1)
                    ch.end()

            def ln_coef(g, between=()):
                between = list(between)
                ch = ln_chain[g]
                y = rs_g[g]
                half, step = nt[g][:, 0, :], nt[g][:, 1, :]
                for _ in range(3):
                    if between:
                        between.pop(0)()
                    ch.wait()
                    for k in range(T2 * LN_SIZE[g]):
                        last = v.scalar_tensor_tensor(step[:, k:k + 1], y[:, k:k + 1], y[:, k:k + 1], half[:, k:k + 1],
                                                      ALU.mult, ALU.mult)
                    ch.did(last)
                    ch.wait()
                    ch.did(v.scalar_tensor_tensor(y[:, :], step, 1.5, y[:, :], ALU.add, ALU.mult))
                ch.wait()
                v.scalar_tensor_tensor(nb_g[g][:, :], mv[g][:, :, 0], -1.0, y[:, :], ALU.mult, ALU.mult).then_inc(ln_cf[g], 1)
                ch.end()

            def tr_low(i, b, lo, hi):
                dve.wait_ge(tr_hi[i], b + 1)
                v.tensor_tensor(lo[:, :, :], two(ps_tr), hi[:, :, :], ALU.subtract).then_inc(tr_lo[i], 1)

            def a_v(b):
                dve.wait_ge(v_rdy, b + 1)
                w(dve, vr_ev, b)
                v.scalar_tensor_tensor(v32[:, :], ps_pt0[0:S2, 0:D], 1 / WS, bv[0:S2, :], ALU.mult, ALU.add).then_inc(v_ev, 1)

            def a_l(b):
                dve.wait_ge(s_ev, b + 1)
                w(dve, sv_rdy, b)
                v.tensor_tensor(l32[:, :], s32[:, :], mT[:, :], ALU.add).then_inc(l_ok, 1)

            def a_x1(b):
                dve.wait_ge(sv_ev, b + 1)
                w(dve, x1_copied, b)
                w(dve, ln_nm[1], b)
                v.scalar_tensor_tensor(x1[:, :, :], o32[:, :, :], G0X, x0[:, :, :], ALU.mult, ALU.add).then_inc(x1_ok, 1)

            def b_lo(hi, lo, hh, hl, j, b):
                dve.wait_ge(hi.sem, hi.nth(j, b))
                v.scalar_tensor_tensor(hl[:, 2 * j:2 * j + 2, :], two(bank[j % 2]), 0.0, hh[:, 2 * j:2 * j + 2, :],
                                       ALU.max, ALU.subtract).then_inc(lo.sem, 1)

            def b_l0(j, b):
                b_lo(l0_hi, l0_lo, h0_h, h0_l, j, b)

            def b_l1(j, b):
                b_lo(l1_hi, l1_lo, h1_h, h1_l, j, b)

            def b_x2(b):
                dve.wait_ge(l2_rdy, b + 1)
                dve.wait_ge(x1_copied, b + 1)
                w(dve, x3_ok, b)
                w(dve, ln_nm[2], b)
                v.scalar_tensor_tensor(x2[:, :, :], two(ps_yo), F0, x1_kept[:, :, :], ALU.mult, ALU.add).then_inc(x2_ok, 1)

            def c_qp(b):
                dve.wait_ge(qp_hi, b + 1)
                v.scalar_tensor_tensor(qp_l[:, :, :], two(ps_m), 1 / WS, qp_h[:, :, :], ALU.mult, ALU.subtract).then_inc(qp_lo, 1)

            def c_argmax(b):
                dve.wait_ge(am_rdy, b + 1)
                cch.start(b)
                plain(1)
                for t in range(T2):
                    last = v.max(am8[:, t, :], ps_tr[:, t * S2:(t + 1) * S2])
                cch.did(last)
                cch.wait()
                plain(2)
                for t in range(T2):
                    last = v.max_index(ami[:, t, :], am8[:, t, :], ps_tr[:, t * S2:(t + 1) * S2])
                cch.did(last)
                cch.wait()
                cch.did(v.tensor_copy(amf[:, :], ami[:, :, 0]))
                cch.wait()
                for t in range(T2):
                    last = v.tensor_scalar(hot[:, t, :], iota_k[:, :], amf[:, t:t + 1], None, ALU.is_equal)
                last.then_inc(hot_ok, 1)

            def c_counts(b):
                dve.wait_ge(cnt_rdy, b + 1)
                v.tensor_scalar(mrow[:, :, :], ps_tr[:, 2 * P:2 * P + S2].unsqueeze(1).to_broadcast([P, HB, S2]),
                                0.0, NEG, ALU.is_equal, ALU.mult).then_inc(mrow_ok, 1)
                cch.did(v.tensor_copy(cnt[:, :], ps_tr[0:S2, 3 * P:3 * P + 1]))
                cch.wait()
                v.tensor_copy(vc_h[:, DH:VW], cnt[:, :])
                dve.wait_ge(handoff, b + 1)
                cch.did(v.tensor_scalar(vc[:, :], vpc[:, :], cnt[:, 0:1], None, ALU.mult))
                cch.wait()
                v.tensor_copy(vc_h[:, 0:DH], vc[:, :]).then_inc(av_dve, 1)
                dve.wait_ge(av_dve, 5 * b + 1)
                v.tensor_tensor(vc_l[:, 0:DH], vc[:, :], vc_h[:, 0:DH], ALU.subtract).then_inc(vc_ok, 1)
                cch.end()

            def c_max(r, b):
                dve.wait_ge(lg_rdy.sem, lg_rdy.nth(r, b))
                lg = ps_lg[:, :, 0:HB * S2].rearrange("p g (h k) -> p g h k", k=S2)
                if r:
                    dve.wait_ge(p_ok.sem, p_ok.nth(r - 1, b))
                else:
                    w(dve, p_ok.sem, p_ok.nth(3, b - 1))
                v.tensor_reduce(rmax[:, :].rearrange("p (g h) -> p g h", g=2), lg, AX, ALU.max).then_inc(mx_dve, 1)
                dve.wait_ge(mx_dve, 4 * b + r + 1)
                v.tensor_tensor(z[:, :, :].rearrange("p (g h) k -> p g h k", g=2), lg,
                                rmax[:, :].rearrange("p (g h) -> p g h", g=2).unsqueeze(3).to_broadcast([P, 2, HB, S2]),
                                ALU.subtract).then_inc(z_ok.sem, 1)

            def c_pt(k, b):
                dve.wait_ge(pt_hi_ok.sem, pt_hi_ok.nth(k, b))
                hh = slice(k % 2 * HB, (k % 2 + 1) * HB)
                v.tensor_tensor(pt_l[:, hh, :], ps_pt[k % 2][0:S2, :].rearrange("p (h n) -> p h n", h=HB),
                                pt_h[:, hh, :], ALU.subtract).then_inc(pt_lo_ok.sem, 1)

            def c_norm(r, b):
                t, c = divmod(r, C2)
                dve.wait_ge(av_rdy.sem, av_rdy.nth(r, b))
                av = ps_m[:, 0:HC * VW].rearrange("p (h n) -> p h n", n=VW)
                v.reciprocal(rden[:, :], av[:, :, DH]).then_inc(av_dve, 1)
                dve.wait_ge(av_dve, 5 * b + r + 2)
                v.tensor_tensor(att[:, t, c * P:(c + 1) * P].rearrange("p (h n) -> p h n", n=DH), av[:, :, 0:DH],
                                rden[:, :].unsqueeze(2).to_broadcast([P, HC, DH]), ALU.mult).then_inc(av_ev.sem, 1)

            def c_x3(b):
                dve.wait_ge(wc_rdy, b + 1)
                w(dve, x4_ok, b)
                v.scalar_tensor_tensor(x3[:, :, :], two(ps_m), G1X, x2[:, :, :], ALU.mult, ALU.add).then_inc(x3_ok, 1)

            def d_max(b):
                dve.wait_ge(rt_rdy, b + 1)
                plain(3)
                for t in range(T2):
                    last = v.max(lt8[:, t, :], ps_pt0[:, t * (E + 1):t * (E + 1) + E])
                last.then_inc(lt_ok, 1)
                dve.wait_ge(lt_ok, b + 1)
                v.tensor_scalar(ltm[:, :], lt8[:, :, 0], -1 / WS, None, ALU.mult).then_inc(rt_max, 1)

            def d_choose(b):
                rch.start(b)
                dve.wait_ge(rt_exp, b + 1)
                plain(4)
                for t in range(T2):
                    last = v.max(e8[:, t, :], ex[:, t, :])
                rch.did(last)
                rch.wait()
                plain(5)
                for t in range(T2):
                    last = v.match_replace(erp[:, t, :], e8[:, t, :], ex[:, t, :], -1.0)
                rch.did(last)
                rch.did(v.tensor_reduce(es8[:, :], e8[:, :, :], AX, ALU.add))
                rch.wait()
                rch.did(v.reciprocal(er8[:, :], es8[:, :]))
                rch.did(v.tensor_scalar(chosen[:, :, :], erp[:, :, :], 0.0, None, ALU.is_lt))
                rch.wait()
                w(dve, xr_out, 16 * b)
                for t in range(T2):
                    last = v.scalar_tensor_tensor(xr[:, t, D:XR], ex[:, t, :], er8[:, t:t + 1], chosen[:, t, :], ALU.mult, ALU.mult)
                last.then_inc(ch_ok, 1)

            def d_pos(b):
                dve.wait_ge(cp_rdy, b + 1)
                rch.did(v.tensor_tensor(pos[:, :, :], ps_tr[:, 0:T2 * E].rearrange("p (t e) -> p t e", t=T2),
                                        carry[:, :].unsqueeze(1).to_broadcast([P, T2, E]), ALU.add))
                rch.wait()
                v.tensor_tensor(carry[:, :], ps_tr[:, T2 * E:(T2 + 1) * E], carry[:, :], ALU.add).then_inc(pos_ev, 1)

            def d_slots(b):
                w(dve, scattered, 16 * T2 * TOPK * b)
                rch.did(v.scalar_tensor_tensor(kept[:, :, :], pos[:, :, :], float(CAP), chosen[:, :, :], ALU.is_lt, ALU.mult))
                rch.did(v.tensor_tensor(key[:, :, :], ebase[:, :].unsqueeze(1).to_broadcast([P, T2, E]), pos[:, :, :], ALU.subtract))
                rch.wait()
                rch.did(v.tensor_tensor(val[:, :, :], key[:, :, :], kept[:, :, :], ALU.mult))
                rch.wait()
                plain(6)
                for t in range(T2):
                    last = v.max(v8[:, t, :], val[:, t, :])
                rch.did(last)
                rch.did(v.tensor_scalar(tokf[:, :], tokf[:, :], float(S), None, ALU.add))
                rch.wait()
                v.tensor_copy(toki[:, :], tokf[:, :]).then_inc(tok_ok, 1)
                v.tensor_scalar(slot[:, :, :], v8[:, :, :], -1.0, float(NT), ALU.mult, ALU.add).then_inc(slots_ok, 1)
                rch.end()

            def d_gu(j, b):
                dve.wait_ge(gu_th.sem, gu_th.nth(j, b))
                two_ = two(bank[j % 2])
                v.scalar_tensor_tensor(ga[:, j, :], th[:, j, :], 1.0, two_[:, 0, :], ALU.add, ALU.mult).then_inc(gu_dve, 1)
                dve.wait_ge(gu_dve, 4 * b + j + 1)
                v.scalar_tensor_tensor(ac[:, j, :], ga[:, j, :], 0.5 / (WS * WS), two_[:, 1, :], ALU.mult, ALU.mult).then_inc(gu_ac.sem, 1)

            def d_ac(j, b):
                dve.wait_ge(ac_hi.sem, ac_hi.nth(j, b))
                v.tensor_tensor(ac_l[:, j, :], ac[:, j, :], ac_h[:, j, :], ALU.subtract).then_inc(ac_lo.sem, 1)

            def d_x4(b):
                dve.wait_ge(dn_rdy, b + 1)
                w(dve, x4_out, 16 * b)
                v.tensor_scalar(sgc[:, :], sgt[:, :], 1.0, G1F, ALU.add, ALU.mult).then_inc(sg_ok, 1)
                dve.wait_ge(sg_ok, b + 1)
                for t in range(T2):
                    last = v.scalar_tensor_tensor(x4[:, t, :], two(ps_yo)[:, t, :], sgc[:, t:t + 1], x3[:, t, :], ALU.mult, ALU.add)
                last.then_inc(x4_ok, 1)

            def first(n, c, m, d):
                if n is not None:
                    for j in range(4):
                        b_l0(j, n)
                if c is not None:
                    c_argmax(c)
                if m is not None:
                    ln_stats(0, m, (0, x0, (x_in, 16 * m + 16), (ln_nm[0], m)))
                if c is not None:
                    c_counts(c)
                if n is not None:
                    b_l1(0, n)
                if d is not None:
                    d_choose(d)
                if c is not None:
                    c_max(0, c)
                if n is not None:
                    b_l1(1, n)
                for r in range(4):
                    if m is not None and r == 2:
                        tr_low(0, m, xt_l[0], xt_h[0])
                    if c is not None:
                        c_pt(2 * r, c)
                        c_pt(2 * r + 1, c)
                        if r < 3:
                            c_max(r + 1, c)
                    if n is not None and r == 1:
                        b_l1(2, n)
                    if c is not None:
                        c_norm(r, c)
                    if d is not None and r == 2:
                        d_pos(d)
                if n is not None:
                    b_l1(3, n)
                if d is not None:
                    d_slots(d)

            def second(n, c, m, d):
                if c is not None:
                    tr_low(4, c, at_l, at_h)
                if m is not None:
                    a_v(m)
                if c is not None:
                    c_x3(c)
                    ln_stats(2, c, (0, x3, (x3_ok, c + 1), (ln_nm[3], c)))
                if m is not None:
                    a_l(m)
                if c is not None:
                    ln_coef(2)
                if m is not None:
                    a_x1(m)
                if n is not None:
                    b_x2(n)
                if c is not None:
                    tr_low(3, c, xt_l[3], xt_h[3])
                srcs = []
                if m is not None:
                    srcs.append((0, x1, (x1_ok, m + 1), (ln_nm[1], m)))
                if n is not None:
                    srcs.append((1, x2, (x2_ok, n + 1), (ln_nm[2], n)))
                if srcs:
                    ln_stats(1, m if n is None else n + 1, *srcs)
                if c is not None:
                    d_max(c)
                if srcs:
                    ln_coef(1, [] if c is None else [lambda: None, lambda: d_gu(0, c)])
                if c is not None:
                    if not srcs:
                        d_gu(0, c)
                    d_gu(1, c)
                    d_ac(0, c)
                if m is not None:
                    tr_low(1, m, xt_l[1], xt_h[1])
                if c is not None:
                    d_ac(1, c)
                    d_gu(2, c)
                if n is not None:
                    tr_low(2, n, xt_l[2], xt_h[2])
                if c is not None:
                    d_gu(3, c)
                    d_ac(2, c)
                    d_ac(3, c)
                if n is not None:
                    c_qp(n)
                if c is not None:
                    d_x4(c)

            first(None, None, 0, None)
            second(None, None, 0, None)
            first(0, None, 1, None)
            second(0, None, 1, None)
            first(1, 0, 2, None)
            second(1, 0, 2, None)
            first(2, 1, 3, 0)
            second(2, 1, 3, 0)
            with dve.Fori(3, NB - 1) as n:
                first(n, n - 1, n + 1, n - 2)
                second(n, n - 1, n + 1, n - 2)
            first(NB - 1, NB - 2, None, NB - 3)
            second(NB - 1, NB - 2, None, NB - 3)
            first(None, NB - 1, None, NB - 2)
            second(None, NB - 1, None, NB - 2)
            first(None, None, None, NB - 1)

            dve.wait_ge(ids_in, 16)
            v.tensor_copy(slots_f[:, :], slots_row[:, :]).then_inc(ids_f, 1)
            dve.wait_ge(ids_t, 1)
            v.tensor_copy(ids[:, :], ps_yo[:, 0:E]).then_inc(ids_ok, 1)
            dve.wait_ge(ids_ok, 1)

            def gather_ids(e, u):
                w(dve, e_tr, e - XD + 1)
                v.tensor_copy(gid[u][:, :], ids[:, bass.ds(e, 1)]).then_inc(e_gid, 1)

            def split_weights(e, u):
                dve.wait_ge(e_wh, e + 1)
                v.scalar_tensor_tensor(ew_l[u][:, :, :], ew[u % 2][:, :, :], WS, ew_h[u][:, :, :], ALU.mult, ALU.subtract).then_inc(e_wl, 1)

            def rows_low(e, u):
                dve.wait_ge(e_trh, e + 1)
                v.tensor_scalar(ewt[u][:, :], xg[u][:, bass.ds(D + e, 1)], sc[:, 7:8], None, ALU.mult).then_inc(e_wt, 1)
                v.tensor_tensor(eg_l[u % 2][:, :, :], ps_eg[u % 2][:, 0:D].rearrange("p (c n) -> p c n", c=C2), eg_h[u % 2][:, :, :],
                                ALU.subtract).then_inc(e_trl, 1)

            def weighted(e, u):
                dve.wait_ge(e_wt, e + 1)
                dve.wait_ge(e_dn, e + 1)
                w(dve, e_out, 16 * (e - 1))
                v.tensor_copy(aid[u][:, :], ids[:, bass.ds(e, 1)]).then_inc(e_aid, 1)
                v.tensor_scalar(ey[u % 2][:, :], ps_lg[:, u % 2, 0:D], ewt[u][:, 0:1], None, ALU.mult).then_inc(e_y, 1)

            def expert(e, u):
                if within(e, XD - 1):
                    gather_ids(e + XD - 1, (u - 1) % XD)
                if within(e, 1):
                    rows_low(e + 1, (u + 1) % XD)
                dve.wait_ge(e_th, e + 1)
                v.scalar_tensor_tensor(ega[u % 2][:, :], eth[u % 2][:, :], 1.0, bank[u % 2][:, 0:P], ALU.add, ALU.mult).then_inc(e_ga, 1)
                dve.wait_ge(e_ga, e + 1)
                v.scalar_tensor_tensor(eac[u % 2][:, :], ega[u % 2][:, :], 0.5 / (WS * WS), bank[u % 2][:, P:2 * P], ALU.mult, ALU.mult).then_inc(e_ac, 1)
                if within(e, -1):
                    weighted(e - 1, (u - 1) % XD)
                dve.wait_ge(e_ach, e + 1)
                v.tensor_tensor(ea_l[u % 2][:, :], eac[u % 2][:, :], ea_h[u % 2][:, :], ALU.subtract).then_inc(e_acl, 1)
                if within(e, 2):
                    split_weights(e + 2, (u + 2) % XD)

            for e in range(XD - 1):
                gather_ids(e, e)
            split_weights(0, 0)
            split_weights(1, 1)
            rows_low(0, 0)
            each_expert(dve, expert)
            weighted(E - 1, (E - 1) % XD)


def kernel(**inputs):
    from concourse import bacc as _bacc
    from concourse.bass_utils import run_bass_kernel_spmd as _run

    a = {k: np.asarray(v) for k, v in inputs.items()}
    f = {
        "x": a["x"],
        "ctxT": a["ctx_1024"].transpose(0, 2, 1),
        "maskT": a["mask_1xSxS2_ff0"][0].T,
        "g_xattn": a["g_xattn"], "g_ffn": a["g_ffn"],
        "wq0": a["L0_xattn_kernel_q"][0, 0], "wk0": a["L0_xattn_kernel_k"][0, 0], "wv0": a["L0_xattn_kernel_v"][0, 0],
        "bq0": a["L0_xattn_bias_q"].reshape(C2, P).T, "bk0": a["L0_xattn_bias_k"].reshape(C2, P).T, "bv0": a["L0_xattn_bias_v"],
        "k0": a["L0_ffn_k0"].view(np.int32), "k1": a["L0_ffn_k1"].view(np.int32), "k2": a["L0_ffn_k2"].view(np.int32),
        "s0": a["L0_ffn_s0"].reshape(1), "s1": a["L0_ffn_s1"].reshape(1), "s2": a["L0_ffn_s2"].reshape(1),
        "wqT1": a["L1_xattn_Wq"].T, "wkvT1": a["L1_xattn_Wkv"].T, "wcT1": a["L1_xattn_Wc"].T,
        "gates_w": np.concatenate([a["L1_ffn_gate_w"], a["L1_ffn_shared_gate_w"]], axis=1),
        "sgu_w": a["L1_ffn_shared_gate_up_w"], "sdown_w": a["L1_ffn_shared_down_w"],
        "egu_w": a["L1_ffn_expert_gate_up_w"], "edown_w": a["L1_ffn_expert_down_w"],
    }
    nc = _bacc.Bacc("TRN2", target_bir_lowering=False, num_devices=1)
    arrays, args = {}, []
    for name, v in f.items():
        v = np.ascontiguousarray(v)
        arrays[f"in_{name}"] = v
        args.append(nc.dram_tensor(f"in_{name}", v.shape, mybir.dt.from_np(v.dtype), kind="ExternalInput").ap())
    out = nc.dram_tensor("out_0", [NT + CAP, D], F32, kind="ExternalOutput").ap()
    xrows = nc.dram_tensor("xrows", [NT, XR], F32, kind="Internal").ap()
    table = nc.dram_tensor("table", [E * CAP, 1], I32, kind="Internal").ap()
    build(nc, *args, out, xrows, table)
    r = _run(nc, [arrays], core_ids=[0])
    return r.results[0]["out_0"][:NT].reshape(NB, S, D)
```

```python
from contextlib import ExitStack

import numpy as np

import concourse.bass as bass
from concourse import mybir

F32 = mybir.dt.float32
F16 = mybir.dt.float16
BF16 = mybir.dt.bfloat16
I32 = mybir.dt.int32
U32 = mybir.dt.uint32
U8 = mybir.dt.uint8
ALU = mybir.AluOpType
ACT = mybir.ActivationFunctionType
AX = mybir.AxisListType.X

P = 128
NB, S, D = 32, 256, 256
S2 = 77
T2, C2 = S // P, D // P
F = 1024
FK = F // P
H, DH = 16, 16
HC = P // DH
HB = HC // 2
VW = DH + 1
E, IE, IS, CAP, TOPK = 64, 128, 512, 128, 8
SK = IS // P
NT = NB * S
XR = D + E
EPS = 1e-5
WS = 64.0
HS = 1.0 / 32
NEG = -1e30
XD = 4
GUESS = float(0x5F3759DF - (2 ** 23 + 2 ** 31) // 2)


def w(eng, sem, value):
    if isinstance(value, int) and value <= 0:
        return
    eng.wait_ge(sem, value)


class Many:

    def __init__(self, sem, per):
        self.sem, self.per = sem, per

    def nth(self, j, b):
        return b * self.per + j + 1


class Steps:

    def __init__(self, eng, sem, per):
        self.eng, self.sem, self.per = eng, sem, per

    def start(self, b):
        self.base, self.k = b * self.per, 0

    def did(self, ins):
        ins.then_inc(self.sem, 1)
        self.k += 1
        assert self.k <= self.per

    def wait(self):
        self.eng.wait_ge(self.sem, self.base + self.k)

    def end(self):
        assert self.k == self.per, (self.k, self.per)


def build(nc, x, ctxT, maskT, g_xattn, g_ffn, wq0, wk0, wv0, bq0, bk0, bv0, k0, k1, k2, s0, s1, s2,
          wqT1, wkvT1, wcT1, gates_w, sgu_w, sdown_w, egu_w, edown_w, out, xrows, table):
    es = ExitStack()
    with es:
        def sb(name, shape, dt=F32):
            return es.enter_context(nc.sbuf_tensor(name, shape, dt))

        def sem(name):
            return es.enter_context(nc.semaphore(name))

        def sems(name, n):
            return [sem(f"{name}{i}") for i in range(n)]

        def many(name, per):
            return Many(sem(name), per)

        bank = [es.enter_context(nc.psum_tensor(f"bank{i}", [P, 512], F32)) for i in range(2)]
        ps_lg = es.enter_context(nc.psum_tensor("ps_lg", [P, 2, 512], F32))
        ps_pt0 = es.enter_context(nc.psum_tensor("ps_pt0", [P, 512], F32))
        ps_m = es.enter_context(nc.psum_tensor("ps_m", [P, 512], F32))
        ps_tr = es.enter_context(nc.psum_tensor("ps_tr", [P, 512], F32))
        ps_yo = es.enter_context(nc.psum_tensor("ps_yo", [P, 512], F32))
        ps_pt = [ps_pt0, ps_yo]
        ps_turned = [ps_tr, ps_tr, ps_pt0, ps_tr, ps_tr]
        ps_eg = [ps_tr, ps_m]

        def two(ap):
            return ap[:, :].rearrange("p (a n) -> p a n", a=2)

        ident = sb("ident", [P, P])
        ones16 = sb("ones16", [P, P], F16)
        before16 = sb("before16", [P, P], F16)
        row0 = sb("row0", [P, P], BF16)
        iota_k = sb("iota_k", [P, S2])
        ebase = sb("ebase", [P, E])
        headmask = sb("headmask", [P, HC])
        pad_in = sb("pad_in", [P, 1])
        threehalf = sb("threehalf", [P, T2])
        tokf = sb("tokf", [P, T2])
        toki = sb("toki", [P, T2], I32)
        sent = sb("sent", [E, CAP], I32)
        sc = sb("sc", [P, 16])
        G0X, F0, G1X, G1F = (sc[:, i:i + 1] for i in range(4))
        raw = sb("raw", [P, 7])
        tg = sb("tg", [P, 4])
        sg = sb("sg", [P, 2])
        ab = sb("ab", [P, 2])
        dve_pad = sb("dve_pad", [P, 16])
        pool_pad = sb("pool_pad", [P, 8])
        stage = sb("stage", [P, 5 * C2 * D + C2 * 2 * DH + C2 * (E + 1)])
        stage_b = [sb(f"stage_b{i}", [P, n // 4], I32) for i, n in enumerate((4 * F, FK * F, FK * D))]
        wq_h, wq_l = sb("wq_h", [P, C2, D], F16), sb("wq_l", [P, C2, D], F16)
        wk_h, wk_l = sb("wk_h", [P, C2, D], F16), sb("wk_l", [P, C2, D], F16)
        VN = D + DH
        wv_h, wv_l = sb("wv_h", [P, C2, VN], F16), sb("wv_l", [P, C2, VN], F16)
        wkr_h, wkr_l = sb("wkr_h", [P, C2, P], F16), sb("wkr_l", [P, C2, P], F16)
        wp_h, wp_l = sb("wp_h", [P, C2, D], F16), sb("wp_l", [P, C2, D], F16)
        wc_h, wc_l = sb("wc_h", [P, C2, D], F16), sb("wc_l", [P, C2, D], F16)
        gw_h, gw_l = sb("gw_h", [P, C2, E + 1], F16), sb("gw_l", [P, C2, E + 1], F16)
        gu_h, gu_l = sb("gu_h", [P, C2, 2 * IS], F16), sb("gu_l", [P, C2, 2 * IS], F16)
        dn_h, dn_l = sb("dn_h", [P, SK, D], F16), sb("dn_l", [P, SK, D], F16)
        wb0 = sb("wb0", [P, C2, F], F16)
        wb1 = sb("wb1", [P, FK, F], F16)
        wb2 = sb("wb2", [P, FK, D], F16)
        bqk = sb("bqk", [P, 2, C2])
        bv = sb("bv", [P, D])
        mT = sb("mT", [S2, S])
        x0 = sb("x0", [P, T2, D])
        ctx = sb("ctx", [P, C2, S2])
        ctx_h, ctx_l = sb("ctx_h", [P, C2, P], F16), sb("ctx_l", [P, C2, P], F16)
        xn = [sb(f"xn{i}", [P, T2, D]) for i in range(3)]
        xt_h = [sb(f"xt{i}_h", [P, C2, S], F16) for i in range(4)]
        xt_l = [sb(f"xt{i}_l", [P, C2, S], F16) for i in range(4)]
        stats = [sb(f"stats{i}", [P, T2, 6]) for i in range(4)]
        mv = [sb(f"mv{i}", [P, T2, 2]) for i in range(4)]
        nt = [sb(f"nt{i}", [P, 2, T2]) for i in range(4)]
        rs = [sb(f"rs{i}", [P, T2]) for i in range(4)]
        nb = [sb(f"nb{i}", [P, T2]) for i in range(4)]
        q32 = sb("q32", [P, C2, S])
        kp32 = sb("kp32", [P, C2, P])
        v32 = sb("v32", [S2, D])
        v32r = sb("v32r", [S2, D])
        vp32 = sb("vp32", [S2, DH])
        kr32 = sb("kr32", [P, S2])
        s32 = sb("s32", [S2, S])
        l32 = sb("l32", [S2, S])
        o32 = sb("o32", [P, T2, D])
        x1 = sb("x1", [P, T2, D])
        x1_kept = sb("x1_kept", [P, T2, D])
        h0_h, h0_l = sb("h0_h", [P, FK, S], F16), sb("h0_l", [P, FK, S], F16)
        h1_h, h1_l = sb("h1_h", [P, FK, S], F16), sb("h1_l", [P, FK, S], F16)
        x2 = sb("x2", [P, T2, D])
        cx_h, cx_l = sb("cx_h", [P, C2, S2], F16), sb("cx_l", [P, C2, S2], F16)
        kr_h, kr_l = sb("kr_h", [P, S2], F16), sb("kr_l", [P, S2], F16)
        kb_h, kb_l = sb("kb_h", [P, HC, S2], F16), sb("kb_l", [P, HC, S2], F16)
        vpc = sb("vpc", [S2, DH])
        qp_h, qp_l = sb("qp_h", [P, C2, S], F16), sb("qp_l", [P, C2, S], F16)
        am8 = sb("am8", [P, T2, 8])
        ami = sb("ami", [P, T2, 8], U32)
        amf = sb("amf", [P, T2])
        hot = sb("hot", [P, T2, S2], F16)
        mrow = sb("mrow", [P, HB, S2], BF16)
        cnt = sb("cnt", [S2, 1])
        vc = sb("vc", [S2, DH])
        vc_h, vc_l = sb("vc_h", [S2, VW], F16), sb("vc_l", [S2, VW], F16)
        rmax = sb("rmax", [P, HC])
        z = sb("z", [P, HC, S2])
        p32 = sb("p32", [P, HC, S2])
        pt_h, pt_l = sb("pt_h", [S2, HC, P], F16), sb("pt_l", [S2, HC, P], F16)
        rden = sb("rden", [P, HC])
        att = sb("att", [P, T2, D])
        at_h, at_l = sb("at_h", [P, C2, S], F16), sb("at_l", [P, C2, S], F16)
        x3 = sb("x3", [P, T2, D])
        xr = sb("xr", [P, T2, XR])
        th = sb("th", [P, IS // P, S])
        ga = sb("ga", [P, 4, S])
        ac = sb("ac", [P, SK, S])
        ac_h, ac_l = sb("ac_h", [P, SK, S], F16), sb("ac_l", [P, SK, S], F16)
        lt8 = sb("lt8", [P, T2, 8])
        ltm = sb("ltm", [P, T2])
        ex = sb("ex", [P, T2, E])
        e8 = sb("e8", [P, T2, 8])
        es8 = sb("es8", [P, T2])
        er8 = sb("er8", [P, T2])
        erp = sb("erp", [P, T2, E])
        chosen = sb("chosen", [P, T2, E], F16)
        sgt = sb("sgt", [P, T2])
        sgc = sb("sgc", [P, T2])
        carry = sb("carry", [P, E])
        pos = sb("pos", [P, T2, E])
        kept = sb("kept", [P, T2, E])
        key = sb("key", [P, T2, E])
        val = sb("val", [P, T2, E])
        v8 = sb("v8", [P, T2, 8])
        slot = sb("slot", [P, T2, 8], I32)
        x4 = sb("x4", [P, T2, D])
        slots_row = sb("slots_row", [E, CAP], I32)
        slots_f = sb("slots_f", [E, CAP])
        ids = sb("ids", [P, E], I32)
        gid = [sb(f"gid{i}", [P, 1], I32) for i in range(XD)]
        aid = [sb(f"aid{i}", [P, 1], I32) for i in range(XD)]
        xg = [sb(f"xg{i}", [P, XR]) for i in range(XD)]
        ew_h = [sb(f"ew{i}_h", [P, 3, D], F16) for i in range(XD)]
        ew_l = [sb(f"ew{i}_l", [P, 3, D], F16) for i in range(XD)]
        ew = [sb(f"ew{i}", [P, 3, D]) for i in range(2)]
        eg_h = [sb(f"eg{i}_h", [P, C2, P], F16) for i in range(2)]
        eg_l = [sb(f"eg{i}_l", [P, C2, P], F16) for i in range(2)]
        eth = [sb(f"eth{i}", [P, P]) for i in range(2)]
        ega = [sb(f"ega{i}", [P, P]) for i in range(2)]
        eac = [sb(f"eac{i}", [P, P]) for i in range(2)]
        ea_h = [sb(f"ea{i}_h", [P, P], F16) for i in range(2)]
        ea_l = [sb(f"ea{i}_l", [P, P], F16) for i in range(2)]
        ewt = [sb(f"ewt{i}", [P, 1]) for i in range(XD)]
        ey = [sb(f"ey{i}", [P, D]) for i in range(2)]

        consts = sem("consts")
        consts2 = sem("consts2")
        split_in, bools_in = sems("split_in", 10), sems("bools_in", 3)
        bools_ok = sem("bools_ok")
        small_dma = sem("small_dma")
        gates_tanh = sem("gates_tanh")
        setup_hi = sem("setup_hi")
        setup_lo = sem("setup_lo")
        setup_dve = sem("setup_dve")
        table_dma = sem("table_dma")
        x_in, ctx_in = sem("x_in"), sem("ctx_in")
        ln_st, ln_pool = sem("ln_st"), sem("ln_pool")
        ln_cf, ln_nm, ln_dve = (sems(n, 4) for n in ("ln_cf", "ln_nm", "ln_dve"))
        tr_rdy, tr_hi, tr_lo = (sems(n, 5) for n in ("tr_rdy", "tr_hi", "tr_lo"))
        ctx_split, kv_rdy, v_rdy = sem("ctx_split"), sem("kv_rdy"), sem("v_rdy")
        x1_copied = sem("x1_copied")
        kp_ev, v_ev, vr_ev, vp_ev = sem("kp_ev"), sem("v_ev"), sem("vr_ev"), sem("vp_ev")
        q_rdy, q_ev, s_rdy, s_ev, l_ok = sem("q_rdy"), sem("q_ev"), sem("s_rdy"), sem("s_ev"), sem("l_ok")
        sv_rdy, sv_ev, x1_ok = sem("sv_rdy"), sem("sv_ev"), sem("x1_ok")
        l0_rdy, l0_hi, l0_lo = (many(n, FK // 2) for n in ("l0_rdy", "l0_hi", "l0_lo"))
        l1_rdy, l1_hi, l1_lo = (many(n, FK // 2) for n in ("l1_rdy", "l1_hi", "l1_lo"))
        l2_rdy, x2_ok = sem("l2_rdy"), sem("x2_ok")
        pad_ok, lt_ok, sg_ok = sem("pad_ok"), sem("lt_ok"), sem("sg_ok")
        cx_ok, kr_hi = sem("cx_ok"), sem("kr_hi")
        handoff, kb_ok, ctx_hi = sem("handoff"), sem("kb_ok"), sem("ctx_hi")
        qp_rdy, qp_hi, qp_lo = sem("qp_rdy"), sem("qp_hi"), sem("qp_lo")
        am_rdy, hot_ok, c_dve = sem("am_rdy"), sem("hot_ok"), sem("c_dve")
        cnt_rdy, mrow_ok, vc_ok = sem("cnt_rdy"), sem("mrow_ok"), sem("vc_ok")
        lg_rdy, z_ok, p_ok = (many(n, 4) for n in ("lg_rdy", "z_ok", "p_ok"))
        pt_rdy, pt_hi_ok, pt_lo_ok = (many(n, 8) for n in ("pt_rdy", "pt_hi_ok", "pt_lo_ok"))
        av_rdy, av_ev = many("av_rdy", 4), many("av_ev", 4)
        av_dve, mx_dve = sem("av_dve"), sem("mx_dve")
        wc_rdy, x3_ok = sem("wc_rdy"), sem("x3_ok")
        rt_rdy, rt_max, rt_exp, rt_dve, ch_ok = (sem(n) for n in ("rt_rdy", "rt_max", "rt_exp", "rt_dve", "ch_ok"))
        cp_rdy, pos_ev, slots_ok, scattered, xr_out = (sem(n) for n in ("cp_rdy", "pos_ev", "slots_ok", "scattered", "xr_out"))
        gu_rdy, gu_th, gu_ac, gu_dve = many("gu_rdy", 4), many("gu_th", 4), many("gu_ac", 4), sem("gu_dve")
        ac_hi, ac_lo = many("ac_hi", 4), many("ac_lo", 4)
        dn_rdy, x4_ok, x4_out, tok_ok = sem("dn_rdy"), sem("x4_ok"), sem("x4_out"), sem("tok_ok")

        e_x, e_w = sems("e_x", XD), sems("e_w", 2)
        ids_in, ids_f, ids_t, ids_ok, e_gid, e_aid, e_out = (
            sem(n) for n in ("ids_in", "ids_f", "ids_t", "ids_ok", "e_gid", "e_aid", "e_out"))
        e_wh, e_wl, e_tr, e_trh, e_trl, e_gu, e_th, e_ga = (
            sem(n) for n in ("e_wh", "e_wl", "e_tr", "e_trh", "e_trl", "e_gu", "e_th", "e_ga"))
        e_ac, e_ach, e_acl, e_dn, e_wt, e_y = (sem(n) for n in ("e_ac", "e_ach", "e_acl", "e_dn", "e_wt", "e_y"))

        def each_expert(eng, step):
            for e in range(XD):
                step(e, e)
            with eng.Fori(1, E // XD - 1) as i:
                for u in range(XD):
                    step(i * XD + u, u)
            for e in range(E - XD, E):
                step(e, e % XD)

        def within(e, ahead):
            return not isinstance(e, int) or 0 <= e + ahead < E

        def fold(ap):
            return ap.rearrange("(c p) n -> p c n", p=P)

        place = [0]

        def staged(src, region=None):
            c, n = src.shape[1], src.shape[2]
            if region is None:
                region = stage[:, place[0]:place[0] + c * n]
                place[0] += c * n
            return region.rearrange("p (c n) -> p c n", c=c)

        splits = [(src, staged(src, region), hi, lo) for src, region, hi, lo in [
            (fold(wq0), None, wq_h[:, :, :], wq_l[:, :, :]),
            (fold(wk0), None, wk_h[:, :, :], wk_l[:, :, :]),
            (fold(wv0), None, wv_h[:, :, 0:D], wv_l[:, :, 0:D]),
            (fold(wkvT1[:, DH:2 * DH]), None, wv_h[:, :, D:VN], wv_l[:, :, D:VN]),
            (fold(wkvT1[:, 0:DH]), None, None, None),
            (fold(wqT1), None, wp_h[:, :, :], wp_l[:, :, :]),
            (fold(wcT1), None, wc_h[:, :, :], wc_l[:, :, :]),
            (fold(gates_w), None, gw_h[:, :, :], gw_l[:, :, :]),
            (fold(sgu_w), stage_b[1][:, :].bitcast(F32), gu_h[:, :, :], gu_l[:, :, :]),
            (fold(sdown_w), stage_b[0][:, :].bitcast(F32), dn_h[:, :, :], dn_l[:, :, :]),
        ]]
        FOR_A, FOR_C, FOR_D = range(0, 5), range(5, 8), range(8, 10)
        bools = [(k0, 4), (k1, FK), (k2, FK)]

        def byte_rows(k):
            return stage_b[k][:, :].bitcast(U8).rearrange("p (c n) -> p c n", c=bools[k][1])

        block = es.enter_context(nc.Block())

        @block.sync
        def _(sp):
            def load_split(k):
                src, dst = splits[k][:2]
                sp.dma_start(dst, src).then_inc(split_in[k], 16)

            def load_bools(k):
                src, c = bools[k]
                sp.dma_start(stage_b[k][:, :].rearrange("p (c n) -> p c n", c=c),
                             src.rearrange("(c p) n -> p c n", p=P)).then_inc(bools_in[k], 16)

            def load_x(b):
                w(sp, x1_ok, b)
                sp.dma_start(x0[:, :, :], x[bass.ds(b, 1)].rearrange("o (t p) d -> p (o t) d", p=P)).then_inc(x_in, 16)

            def load_ctx(b):
                w(sp, ctx_split, b)
                sp.dma_start(ctx[:, :, :], ctxT[bass.ds(b, 1)].rearrange("o (c p) k -> p (o c) k", p=P)).then_inc(ctx_in, 16)

            def store_rows(b):
                sp.wait_ge(ch_ok, b + 1)
                sp.wait_ge(ln_nm[3], b + 1)
                sp.dma_start(xrows[bass.ds(b * S, S)].rearrange("(t p) n -> p t n", p=P), xr[:, :, :]).then_inc(xr_out, 16)

            def store_x4(b):
                sp.wait_ge(x4_ok, b + 1)
                sp.dma_start(out[bass.ds(b * S, S)].rearrange("(t p) n -> p t n", p=P), x4[:, :, :]).then_inc(x4_out, 16)

            load_x(0)
            load_ctx(0)
            for k in FOR_A:
                load_split(k)
            small = [(raw[:, 0:2], g_xattn), (raw[:, 2:4], g_ffn), (raw[:, 4:5], s0), (raw[:, 5:6], s1),
                     (raw[:, 6:7], s2), (bv[:, :], bv0)]
            for dst, src in small:
                sp.dma_start(dst, src.partition_broadcast(P)).then_inc(small_dma, 16)
            sp.dma_start(bqk[:, 0, :], bq0).then_inc(small_dma, 16)
            sp.dma_start(bqk[:, 1, :], bk0).then_inc(small_dma, 16)
            sp.dma_start(mT[:, :], maskT).then_inc(small_dma, 16)
            for k in range(3):
                load_bools(k)
            for k in FOR_C:
                load_split(k)
            sp.wait_ge(consts, 1)
            sp.dma_start(table.rearrange("(e c) o -> e (c o)", c=CAP), sent[:, :]).then_inc(table_dma, 16)
            sp.wait_ge(consts2, 25)
            sp.dma_start(out[NT:NT + CAP], xg[0][:, 0:D]).then_inc(table_dma, 16)
            sp.wait_ge(bools_ok, 1)
            load_split(9)
            sp.wait_ge(bools_ok, 2)
            load_split(8)
            load_x(1)
            load_ctx(1)
            load_x(2)
            load_ctx(2)
            load_x(3)
            load_ctx(3)
            store_x4(0)
            store_rows(0)
            load_x(4)
            with sp.Fori(3, NB - 2) as n:
                load_ctx(n + 1)
                store_x4(n - 2)
                store_rows(n - 2)
                load_x(n + 2)
            load_ctx(NB - 1)
            for b in range(NB - 4, NB):
                store_x4(b)
                store_rows(b)
            sp.wait_ge(scattered, 16 * T2 * TOPK * NB)

            sp.dma_start(slots_row[:, :], table.rearrange("(e c) o -> e (c o)", c=CAP)).then_inc(ids_in, 16)

            def load_weights(e, u):
                w(sp, e_wl, e - 1)
                sp.dma_start(ew[u % 2][:, 0:2, :], egu_w[bass.ds(e, 1)].rearrange("o (c p) n -> p (o c) n", p=P)).then_inc(e_w[u % 2], 16)
                sp.dma_start(ew[u % 2][:, 2, :], edown_w[bass.ds(e, 1)].rearrange("o p n -> p (o n)")).then_inc(e_w[u % 2], 16)

            each_expert(sp, load_weights)
            sp.wait_ge(e_out, 16 * E)

        @block.gpsimd
        def _(pool):
            g = nc.gpsimd
            g.iota(sent[:, :], pattern=[[1, CAP]], base=NT, channel_multiplier=0).then_inc(consts, 1)
            g.memset(ident[:, :], 0.0).then_inc(consts2, 1)
            g.memset(before16[:, :], 1.0).then_inc(consts2, 1)
            g.memset(row0[:, :], 1.0).then_inc(consts2, 1)
            g.memset(headmask[:, :], 1.0).then_inc(consts2, 1)
            pool.wait_ge(consts2, 4)
            g.affine_select(out=ident[:, :], in_=ident[:, :], compare_op=ALU.not_equal, fill=1.0,
                            base=0, pattern=[[-1, P]], channel_multiplier=1).then_inc(consts2, 1)
            g.affine_select(out=before16[:, :], in_=before16[:, :], compare_op=ALU.is_gt, fill=0.0,
                            base=0, pattern=[[1, P]], channel_multiplier=-1).then_inc(consts2, 1)
            g.affine_select(out=row0[:, :], in_=row0[:, :], compare_op=ALU.is_equal, fill=0.0,
                            base=0, pattern=[[0, P]], channel_multiplier=1).then_inc(consts2, 1)
            g.affine_select(out=headmask[:, :], in_=headmask[:, :], compare_op=ALU.is_ge, fill=0.0,
                            base=0, pattern=[[-DH, HC]], channel_multiplier=1).then_inc(consts2, 1)
            pool.wait_ge(consts2, 8)
            g.affine_select(out=headmask[:, :], in_=headmask[:, :], compare_op=ALU.is_gt, fill=0.0,
                            base=DH, pattern=[[DH, HC]], channel_multiplier=-1).then_inc(consts2, 1)
            g.iota(iota_k[:, :], pattern=[[1, S2]], base=0, channel_multiplier=0,
                   allow_small_or_imprecise_dtypes=True).then_inc(consts2, 1)
            g.iota(ebase[:, :], pattern=[[-CAP, E]], base=NT, channel_multiplier=0,
                   allow_small_or_imprecise_dtypes=True).then_inc(consts2, 1)
            g.iota(tokf[:, :], pattern=[[P, T2]], base=-S, channel_multiplier=1,
                   allow_small_or_imprecise_dtypes=True).then_inc(consts2, 1)
            g.memset(ones16[:, :], 1.0).then_inc(consts2, 1)
            g.memset(pad_in[:, :], 0.0).then_inc(consts2, 1)
            g.memset(threehalf[:, :], 1.5).then_inc(consts2, 1)
            g.memset(carry[:, :], 0.0).then_inc(consts2, 1)
            g.memset(ctx_h[:, :, :], 0.0).then_inc(consts2, 1)
            g.memset(ctx_l[:, :, :], 0.0).then_inc(consts2, 1)
            for rows in xg:
                g.memset(rows[:, :], 0.0).then_inc(consts2, 1)
            g.memset(vc_h[:, :], 0.0).then_inc(consts2, 1)
            g.memset(vc_l[:, :], 0.0).then_inc(consts2, 1)

            g.memset(pool_pad[:, :], 0.0).then_inc(consts2, 1)
            pool.wait_ge(consts2, 25)

            def plain(site):
                return g.tensor_tensor(pool_pad[:, site:site + 1], pad_in[:, :], pad_in[:, :], ALU.mult)

            def split_ctx(b):
                pool.wait_ge(ctx_in, 16 * b + 16)
                w(pool, v_rdy, b)
                w(pool, cx_ok, 2 * b)
                plain(0)
                g.tensor_copy(ctx_h[:, :, 0:S2], ctx[:, :, :]).then_inc(ctx_hi, 1)
                pool.wait_ge(ctx_hi, b + 1)
                g.tensor_tensor(ctx_l[:, :, 0:S2], ctx[:, :, :], ctx_h[:, :, 0:S2], ALU.subtract).then_inc(ctx_split, 1)

            def take_ctx(b):
                pool.wait_ge(ctx_split, b + 1)
                w(pool, am_rdy, b)
                plain(7)
                g.tensor_copy(cx_h[:, :, :], ctx_h[:, :, 0:S2]).then_inc(cx_ok, 1)
                g.tensor_copy(cx_l[:, :, :], ctx_l[:, :, 0:S2]).then_inc(cx_ok, 1)

            def take_keys(b):
                pool.wait_ge(kp_ev, b + 1)
                pool.wait_ge(vp_ev, b + 1)
                w(pool, lg_rdy.sem, lg_rdy.nth(3, b - 1))
                w(pool, vc_ok, b)
                plain(1)
                g.tensor_copy(vpc[:, :], vp32[:, :]).then_inc(kr_hi, 1)
                g.tensor_copy(kr_h[:, :], kr32[:, :]).then_inc(kr_hi, 1)
                pool.wait_ge(kr_hi, 2 * b + 2)
                g.tensor_tensor(kr_l[:, :], kr32[:, :], kr_h[:, :], ALU.subtract).then_inc(handoff, 1)
                hm = headmask[:, :].unsqueeze(2).to_broadcast([P, HC, S2])
                pool.wait_ge(handoff, b + 1)
                g.tensor_tensor(kb_h[:, :, :], kr_h[:, :].unsqueeze(1).to_broadcast([P, HC, S2]), hm, ALU.mult).then_inc(kb_ok, 1)
                g.tensor_tensor(kb_l[:, :, :], kr_l[:, :].unsqueeze(1).to_broadcast([P, HC, S2]), hm, ALU.mult).then_inc(kb_ok, 1)

            def scatter(b):
                pool.wait_ge(slots_ok, b + 1)
                pool.wait_ge(tok_ok, b + 1)
                if not isinstance(b, int):
                    plain(0)
                for t in range(T2):
                    for k in range(TOPK):
                        g.indirect_dma_start(
                            out=table, out_offset=bass.IndirectOffsetOnAxis(ap=slot[:, t, k:k + 1], axis=0),
                            in_=toki[:, t:t + 1], in_offset=None, bounds_check=NT - 1, oob_is_err=False,
                        ).then_inc(scattered, 16)

            def keep_x1(b):
                pool.wait_ge(x1_ok, b + 1)
                w(pool, x2_ok, b)
                if not isinstance(b, int):
                    plain(2)
                g.tensor_copy(x1_kept[:, :, :], x1[:, :, :]).then_inc(x1_copied, 1)

            norm_chain = Steps(pool, ln_pool, 13)

            def ln_norm(b):
                pool.wait_ge(ln_st, b + 1)
                w(pool, tr_rdy[0], b)
                ch = norm_chain
                ch.start(b)
                y, half, step = rs[0][:, :], nt[0][:, 0, :], nt[0][:, 1, :]
                for k in range(3):
                    if k:
                        ch.wait()
                    ch.did(g.tensor_tensor(step, y, y, ALU.mult))
                    ch.wait()
                    ch.did(g.tensor_tensor(step, step, half, ALU.mult))
                    ch.wait()
                    ch.did(g.tensor_tensor(step, step, threehalf[:, :], ALU.add))
                    ch.wait()
                    ch.did(g.tensor_tensor(y, step, y, ALU.mult))
                ch.wait()
                ch.did(g.tensor_tensor(nb[0][:, :], mv[0][:, :, 0], y, ALU.mult))
                ch.wait()
                plain(2)
                for t in range(T2):
                    last = g.tensor_scalar(xn[0][:, t, :], x0[:, t, :], y[:, t:t + 1], nb[0][:, t:t + 1], ALU.mult, ALU.subtract)
                last.then_inc(ln_nm[0], 1)
                ch.end()

            def rows(n, last=False):
                take_ctx(n)
                if not last:
                    split_ctx(n + 1)
                    ln_norm(n + 1)
                take_keys(n)

            split_ctx(0)
            ln_norm(0)
            keep_x1(0)
            rows(0)
            keep_x1(1)
            rows(1)
            keep_x1(2)
            rows(2)
            pool.wait_ge(table_dma, 32)
            scatter(0)
            keep_x1(3)
            with pool.Fori(3, NB - 1) as n:
                rows(n)
                scatter(n - 2)
                keep_x1(n + 1)
            rows(NB - 1, last=True)
            for b in range(NB - 3, NB):
                scatter(b)
            pool.wait_ge(xr_out, 16 * NB)
            pool.wait_ge(x4_out, 16 * NB)

            def gather(e, u):
                pool.wait_ge(e_gid, e + 1)
                w(pool, e_tr, e - XD + 1)
                w(pool, e_wt, e - XD + 1)
                if not isinstance(e, int):
                    plain(3).then_inc(pad_ok, 1)
                g.indirect_dma_start(
                    out=xg[u][:, :], out_offset=None, in_=xrows,
                    in_offset=bass.IndirectOffsetOnAxis(ap=gid[u][:, 0:1], axis=0),
                    bounds_check=NT - 1, oob_is_err=False).then_inc(e_x[u], 16)

            def add_out(e, u):
                pool.wait_ge(e_y, e + 1)
                pool.wait_ge(e_aid, e + 1)
                w(pool, e_out, 16 * e)
                if not isinstance(e, int):
                    plain(4).then_inc(pad_ok, 1)
                g.indirect_dma_start(
                    out=out, out_offset=bass.IndirectOffsetOnAxis(ap=aid[u][:, 0:1], axis=0),
                    in_=ey[u % 2][:, :], in_offset=None, bounds_check=NT + CAP - 1, oob_is_err=True,
                    compute_op=ALU.add).then_inc(e_out, 16)

            g.memset(pool_pad[:, 3:5], 0.0).then_inc(pad_ok, 2)
            for e in range(XD - 1):
                gather(e, e)

            def step(e, u):
                if not isinstance(e, int):
                    pool.wait_ge(pad_ok, 2 * (e - XD + 1))
                if within(e, XD - 1):
                    gather(e + XD - 1, (u - 1) % XD)
                if within(e, -1):
                    add_out(e - 1, (u - 1) % XD)

            each_expert(pool, step)
            add_out(E - 1, (E - 1) % XD)

        @block.scalar
        def _(act):
            a = nc.scalar
            def split_high(ks):
                for k in ks:
                    src, landed, hi, lo = splits[k]
                    act.wait_ge(split_in[k], 16)
                    if hi is None:
                        for h in range(HC):
                            last = a.activation(wkr_h[:, :, h * DH:(h + 1) * DH], landed, ACT.Copy, scale=WS)
                        last.then_inc(setup_hi, 1)
                    else:
                        a.activation(hi, landed, ACT.Copy, scale=WS).then_inc(setup_hi, 1)

            split_high(FOR_A)
            act.wait_ge(small_dma, 16 * 9)
            a.activation(tg[:, :], raw[:, 0:4], ACT.Tanh).then_inc(gates_tanh, 1)
            act.wait_ge(consts2, 25)

            def ln_norm(i, b, src, dst):
                act.wait_ge(ln_cf[i], b + 1)
                for t in range(T2):
                    ins = a.activation(dst[:, t, 0:D], src[:, t, :], ACT.Identity, bias=nb[i][:, t:t + 1], scale=rs[i][:, t:t + 1])
                ins.then_inc(ln_nm[i], 1)

            def tr_high(i, b, dst):
                act.wait_ge(tr_rdy[i], b + 1)
                a.activation(dst[:, :, :], two(ps_turned[i]), ACT.Copy).then_inc(tr_hi[i], 1)

            def a_kv(b):
                act.wait_ge(kv_rdy, b + 1)
                w(act, s_rdy, b)
                w(act, handoff, b)
                for c in range(C2):
                    a.activation(kp32[:, c, :], ps_lg[:, 0, c * P:(c + 1) * P], ACT.Relu, bias=bqk[:, 1, c:c + 1], scale=1 / WS)
                a.activation(kr32[:, :], ps_lg[:, 0, 2 * P:2 * P + S2], ACT.Copy, scale=1 / WS).then_inc(kp_ev, 1)

            def a_vals(b):
                act.wait_ge(v_ev, b + 1)
                a.activation(vp32[:, :], ps_pt0[0:S2, D:VN], ACT.Copy, scale=1 / WS).then_inc(vp_ev, 1)
                w(act, sv_rdy, b)
                a.activation(v32r[:, :], v32[:, :], ACT.Relu).then_inc(vr_ev, 1)

            def a_q(b):
                act.wait_ge(q_rdy, b + 1)
                for c in range(C2):
                    ins = a.activation(q32[:, c, :], ps_lg[:, 1, c * S:(c + 1) * S], ACT.Relu, bias=bqk[:, 0, c:c + 1], scale=1 / WS)
                ins.then_inc(q_ev, 1)

            def a_s(b):
                act.wait_ge(s_rdy, b + 1)
                w(act, l_ok, b)
                a.activation(s32[:, :], ps_lg[0:S2, 0, 0:S], ACT.Relu, scale=1 / 16.0).then_inc(s_ev, 1)

            def a_sv(b):
                act.wait_ge(sv_rdy, b + 1)
                w(act, x1_ok, b)
                a.activation(o32[:, :, :], ps_lg[:, 1, :].rearrange("p (t n) -> p t n", t=T2), ACT.Relu).then_inc(sv_ev, 1)

            def b_l0(j, b):
                act.wait_ge(l0_rdy.sem, l0_rdy.nth(j, b))
                a.activation(h0_h[:, 2 * j:2 * j + 2, :], two(bank[j % 2]), ACT.Relu).then_inc(l0_hi.sem, 1)

            def b_l1(j, b):
                act.wait_ge(l1_rdy.sem, l1_rdy.nth(j, b))
                w(act, l2_rdy, b)
                a.activation(h1_h[:, 2 * j:2 * j + 2, :], two(bank[j % 2]), ACT.Relu).then_inc(l1_hi.sem, 1)

            def c_qp(b):
                act.wait_ge(qp_rdy, b + 1)
                a.activation(qp_h[:, :, :], two(ps_m), ACT.Copy, scale=1 / WS).then_inc(qp_hi, 1)

            def c_exp(r, b):
                act.wait_ge(z_ok.sem, z_ok.nth(r, b))
                if r:
                    act.wait_ge(pt_rdy.sem, pt_rdy.nth(2 * r - 1, b))
                else:
                    w(act, pt_rdy.sem, pt_rdy.nth(7, b - 1))
                a.activation(p32[:, :, :], z[:, :, :], ACT.Exp, scale=1 / float(np.sqrt(DH))).then_inc(p_ok.sem, 1)

            def c_pt(k, b):
                act.wait_ge(pt_rdy.sem, pt_rdy.nth(k, b))
                a.activation(pt_h[:, k % 2 * HB:(k % 2 + 1) * HB, :], ps_pt[k % 2][0:S2, :].rearrange("p (h n) -> p h n", h=HB),
                             ACT.Copy).then_inc(pt_hi_ok.sem, 1)

            def d_route(b):
                act.wait_ge(rt_max, b + 1)
                w(act, ch_ok, b)
                w(act, x4_ok, b)
                for t in range(T2):
                    a.activation(ex[:, t, :], ps_pt0[:, t * (E + 1):t * (E + 1) + E], ACT.Exp, bias=ltm[:, t:t + 1], scale=1 / WS)
                a.activation(sgt[:, :], ps_pt0[:, 0:T2 * (E + 1)].rearrange("p (t n) -> p t n", t=T2)[:, :, E],
                             ACT.Tanh, scale=0.5 / WS).then_inc(rt_exp, 1)

            def d_gu(j, b):
                act.wait_ge(gu_rdy.sem, gu_rdy.nth(j, b))
                w(act, gu_ac.sem, gu_ac.nth(j, b - 1))
                a.activation(th[:, j, :], bank[j % 2][:, 0:S], ACT.Tanh, scale=0.5 / WS).then_inc(gu_th.sem, 1)

            def d_ac(j, b):
                act.wait_ge(gu_ac.sem, gu_ac.nth(j, b))
                w(act, dn_rdy, b)
                a.activation(ac_h[:, j, :], ac[:, j, :], ACT.Copy).then_inc(ac_hi.sem, 1)

            def first(n, c, m, d):
                if n is not None:
                    w(act, l1_rdy.sem, l1_rdy.nth(3, n - 1))
                    b_l0(0, n)
                    b_l0(1, n)
                if c is not None:
                    tr_high(2, c, xt_h[2])
                if n is not None:
                    b_l0(2, n)
                    b_l0(3, n)
                if c is not None:
                    c_qp(c)
                if n is not None:
                    b_l1(0, n)
                if c is not None:
                    c_exp(0, c)
                if n is not None:
                    b_l1(1, n)
                for r in range(4):
                    if c is not None:
                        c_pt(2 * r, c)
                        c_pt(2 * r + 1, c)
                        if r < 3:
                            c_exp(r + 1, c)
                    if n is not None and r == 1:
                        b_l1(2, n)
                    if m is not None and r == 1:
                        tr_high(0, m, xt_h[0])
                if n is not None:
                    b_l1(3, n)

            def second(n, c, m, d):
                if m is not None:
                    a_q(m)
                if c is not None:
                    tr_high(4, c, at_h)
                if m is not None:
                    a_kv(m)
                    a_vals(m)
                    a_s(m)
                    a_sv(m)
                if c is not None:
                    w(act, xr_out, 16 * c)
                    ln_norm(3, c, x3, xr)
                    tr_high(3, c, xt_h[3])
                    d_gu(0, c)
                if m is not None:
                    ln_norm(1, m, x1, xn[1])
                if c is not None:
                    d_gu(1, c)
                if m is not None:
                    tr_high(1, m, xt_h[1])
                if c is not None:
                    d_ac(0, c)
                    d_ac(1, c)
                    d_gu(2, c)
                    d_route(c)
                    d_gu(3, c)
                    d_ac(2, c)
                    d_ac(3, c)
                if n is not None:
                    ln_norm(2, n, x2, xn[2])

            first(None, None, 0, None)
            second(None, None, 0, None)
            split_high(FOR_C)
            first(0, None, 1, None)
            second(0, None, 1, None)
            split_high(FOR_D)
            first(1, 0, 2, None)
            second(1, 0, 2, None)
            first(2, 1, 3, 0)
            second(2, 1, 3, 0)
            with act.Fori(3, NB - 1) as n:
                first(n, n - 1, n + 1, n - 2)
                second(n, n - 1, n + 1, n - 2)
            first(NB - 1, NB - 2, None, NB - 3)
            second(NB - 1, NB - 2, None, NB - 3)
            first(None, NB - 1, None, NB - 2)
            second(None, NB - 1, None, NB - 2)
            first(None, None, None, NB - 1)

            def split_weights(e, u):
                act.wait_ge(e_w[u % 2], (e - u % 2) * 16 + 32)
                w(act, e_dn, e - XD + 1)
                a.activation(ew_h[u][:, :, :], ew[u % 2][:, :, :], ACT.Copy, scale=WS).then_inc(e_wh, 1)

            def rows_high(e, u):
                act.wait_ge(e_tr, e + 1)
                w(act, e_gu, e - 1)
                a.activation(eg_h[u % 2][:, :, :], ps_eg[u % 2][:, 0:D].rearrange("p (c n) -> p c n", c=C2), ACT.Copy).then_inc(e_trh, 1)

            def expert(e, u):
                if within(e, 1):
                    rows_high(e + 1, (u + 1) % XD)
                act.wait_ge(e_gu, e + 1)
                w(act, e_ga, e - 1)
                a.activation(eth[u % 2][:, :], bank[u % 2][:, 0:P], ACT.Tanh, scale=0.5 / WS).then_inc(e_th, 1)
                act.wait_ge(e_ac, e + 1)
                w(act, e_dn, e - 1)
                a.activation(ea_h[u % 2][:, :], eac[u % 2][:, :], ACT.Copy).then_inc(e_ach, 1)
                if within(e, 2):
                    split_weights(e + 2, (u + 2) % XD)

            split_weights(0, 0)
            split_weights(1, 1)
            rows_high(0, 0)
            each_expert(act, expert)

        @block.tensor
        def _(pe):
            mm = nc.tensor.matmul

            def three(out_, parts, start=True, stop=True):
                seq = [(sh, mh) for sh, sl, mh, ml in parts] + [(sh, ml) for sh, sl, mh, ml in parts] \
                    + [(sl, mh) for sh, sl, mh, ml in parts]
                for i, (s_, m_) in enumerate(seq):
                    ins = mm(out_, s_, m_, start=(start and i == 0), stop=(stop and i == len(seq) - 1))
                return ins

            def transposes(i, b, src):
                pe.wait_ge(ln_nm[i], b + 1)
                for t in range(T2):
                    for c in range(C2):
                        ins = nc.tensor.transpose(two(ps_turned[i])[:, c, t * P:(t + 1) * P], src[:, t, c * P:(c + 1) * P], ident[:, :])
                ins.then_inc(tr_rdy[i], 1)

            def a_kv(b):
                pe.wait_ge(ctx_split, b + 1)
                for m in range(C2):
                    three(ps_lg[:, 0, m * P:(m + 1) * P],
                          [(wk_h[:, c, m * P:(m + 1) * P], wk_l[:, c, m * P:(m + 1) * P], ctx_h[:, c, :], ctx_l[:, c, :]) for c in range(C2)])
                three(ps_lg[:, 0, 2 * P:3 * P],
                      [(wkr_h[:, c, :], wkr_l[:, c, :], ctx_h[:, c, :], ctx_l[:, c, :]) for c in range(C2)]).then_inc(kv_rdy, 1)

            def a_vals(b):
                three(ps_pt0[:, 0:VN],
                      [(ctx_h[:, c, :], ctx_l[:, c, :], wv_h[:, c, :], wv_l[:, c, :]) for c in range(C2)]).then_inc(v_rdy, 1)

            def feature_major(dst, wh, wl, xh, xl):
                for m in range(C2):
                    ins = three(dst[:, m, :],
                                [(wh[:, c, m * P:(m + 1) * P], wl[:, c, m * P:(m + 1) * P], xh[:, c, :], xl[:, c, :]) for c in range(C2)])
                return ins

            def a_q(b):
                pe.wait_ge(tr_lo[0], b + 1)
                feature_major(ps_lg[:, 1, :].rearrange("p (a n) -> p a n", a=2), wq_h, wq_l, xt_h[0], xt_l[0]).then_inc(q_rdy, 1)

            def a_s(b):
                pe.wait_ge(kp_ev, b + 1)
                pe.wait_ge(q_ev, b + 1)
                for c in range(C2):
                    ins = mm(ps_lg[:, 0, 0:S], kp32[:, c, :], q32[:, c, :], start=(c == 0), stop=(c == C2 - 1))
                ins.then_inc(s_rdy, 1)

            def a_sv(b):
                pe.wait_ge(l_ok, b + 1)
                pe.wait_ge(vr_ev, b + 1)
                for t in range(T2):
                    ins = mm(ps_lg[:, 1, t * D:(t + 1) * D], l32[:, t * P:(t + 1) * P], v32r[:, :], start=True, stop=True)
                ins.then_inc(sv_rdy, 1)

            def b_l0(j, b):
                if j == 0:
                    pe.wait_ge(tr_lo[1], b + 1)
                    w(pe, gu_ac.sem, gu_ac.nth(2, b - 2))
                elif j == 1:
                    w(pe, gu_ac.sem, gu_ac.nth(3, b - 2))
                else:
                    pe.wait_ge(l0_lo.sem, l0_lo.nth(j - 2, b))
                for m in (2 * j, 2 * j + 1):
                    for k, (s_, m_) in enumerate([(wb0[:, c, m * P:(m + 1) * P], xp[:, c, :]) for xp in (xt_h[1], xt_l[1]) for c in range(C2)]):
                        ins = mm(two(bank[j % 2])[:, m % 2, :], s_, m_, start=(k == 0), stop=(k == 3))
                ins.then_inc(l0_rdy.sem, 1)

            def b_l1(m, b):
                j = m // 2
                if m % 2 == 0:
                    if j < 2:
                        pe.wait_ge(l0_lo.sem, l0_lo.nth(j + 2, b))
                        pe.wait_ge(l0_lo.sem, l0_lo.nth(3, b))
                    else:
                        pe.wait_ge(l1_lo.sem, l1_lo.nth(j - 2, b))
                for i, hp in enumerate((h0_h, h0_l)):
                    for k in range(FK):
                        ins = mm(two(bank[j % 2])[:, m % 2, :], wb1[:, k, m * P:(m + 1) * P], hp[:, k, :],
                                 start=(i == 0 and k == 0), stop=(i == 1 and k == FK - 1))
                if m % 2:
                    ins.then_inc(l1_rdy.sem, 1)

            def b_l2(t, b):
                if t == 0:
                    pe.wait_ge(l1_lo.sem, l1_lo.nth(3, b))
                    w(pe, pt_lo_ok.sem, pt_lo_ok.nth(7, b - 1))
                for i, hp in enumerate((h1_h, h1_l)):
                    for k in range(FK):
                        ins = mm(two(ps_yo)[:, t, :], hp[:, k, t * P:(t + 1) * P], wb2[:, k, :],
                                 start=(i == 0 and k == 0), stop=(i == 1 and k == FK - 1))
                if t == T2 - 1:
                    ins.then_inc(l2_rdy, 1)

            def c_qp(b):
                pe.wait_ge(tr_lo[2], b + 1)
                feature_major(two(ps_m), wp_h, wp_l, xt_h[2], xt_l[2]).then_inc(qp_rdy, 1)

            def c_am(b):
                pe.wait_ge(qp_lo, b + 1)
                pe.wait_ge(cx_ok, 2 * b + 2)
                for t in range(T2):
                    tt = slice(t * P, (t + 1) * P)
                    ins = three(ps_tr[:, t * S2:(t + 1) * S2],
                                [(qp_h[:, c, tt], qp_l[:, c, tt], cx_h[:, c, :], cx_l[:, c, :]) for c in range(C2)])
                ins.then_inc(am_rdy, 1)

            def c_cnt(b):
                pe.wait_ge(hot_ok, b + 1)
                for t in range(T2):
                    mm(ps_tr[:, 2 * P:2 * P + S2], ones16[:, :], hot[:, t, :], start=(t == 0), stop=(t == T2 - 1))
                for t in range(T2):
                    ins = mm(ps_tr[0:S2, 3 * P:3 * P + 1], hot[:, t, :], ones16[:, 0:1], start=(t == 0), stop=(t == T2 - 1))
                ins.then_inc(cnt_rdy, 1)

            def c_lg(r, b):
                t, c = divmod(r, C2)
                if r == 0:
                    pe.wait_ge(kb_ok, 2 * b + 2)
                    pe.wait_ge(mrow_ok, b + 1)
                else:
                    pe.wait_ge(z_ok.sem, z_ok.nth(r - 1, b))
                tt = slice(t * P, (t + 1) * P)
                for g_ in range(2):
                    dst = ps_lg[:, g_, 0:HB * S2]
                    hh = slice(g_ * HB, (g_ + 1) * HB)
                    mm(dst, row0[:, :], mrow[:, :, :], start=True, stop=False)
                    ins = three(dst, [(qp_h[:, c, tt], qp_l[:, c, tt], kb_h[:, hh, :], kb_l[:, hh, :])], start=False)
                ins.then_inc(lg_rdy.sem, 1)

            def c_pt(k, b):
                if k % 2 == 0:
                    pe.wait_ge(p_ok.sem, p_ok.nth(k // 2, b))
                if k >= 2:
                    pe.wait_ge(pt_lo_ok.sem, pt_lo_ok.nth(k - 2, b))
                elif k == 0:
                    w(pe, rt_exp, b)
                else:
                    w(pe, x4_ok, b)
                for h in range(HB):
                    ins = nc.tensor.transpose(ps_pt[k % 2][0:S2, h * P:(h + 1) * P], p32[:, k % 2 * HB + h, :], ident[:, :])
                ins.then_inc(pt_rdy.sem, 1)

            def c_av(r, b):
                pe.wait_ge(pt_lo_ok.sem, pt_lo_ok.nth(2 * r, b))
                pe.wait_ge(pt_lo_ok.sem, pt_lo_ok.nth(2 * r + 1, b))
                if r == 0:
                    pe.wait_ge(vc_ok, b + 1)
                else:
                    pe.wait_ge(av_ev.sem, av_ev.nth(r - 1, b))
                for h in range(HC):
                    ins = three(ps_m[:, h * VW:(h + 1) * VW], [(pt_h[:, h, :], pt_l[:, h, :], vc_h[:, :], vc_l[:, :])])
                ins.then_inc(av_rdy.sem, 1)

            def c_att(b):
                pe.wait_ge(av_ev.sem, av_ev.nth(3, b))
                for t in range(T2):
                    for c in range(C2):
                        ins = nc.tensor.transpose(two(ps_tr)[:, c, t * P:(t + 1) * P], att[:, t, c * P:(c + 1) * P], ident[:, :])
                ins.then_inc(tr_rdy[4], 1)

            def token_major(dst, xh, xl, wh, wl, kk):
                for t in range(T2):
                    tt = slice(t * P, (t + 1) * P)
                    ins = three(dst[:, t, :], [(xh[:, c, tt], xl[:, c, tt], wh[:, c, :], wl[:, c, :]) for c in range(kk)])
                return ins

            def c_wc(b):
                pe.wait_ge(tr_lo[4], b + 1)
                token_major(two(ps_m), at_h, at_l, wc_h, wc_l, C2).then_inc(wc_rdy, 1)

            def d_route(b):
                pe.wait_ge(tr_lo[3], b + 1)
                pe.wait_ge(pt_lo_ok.sem, pt_lo_ok.nth(6, b))
                token_major(ps_pt0[:, 0:T2 * (E + 1)].rearrange("p (t n) -> p t n", t=T2),
                            xt_h[3], xt_l[3], gw_h, gw_l, C2).then_inc(rt_rdy, 1)

            def d_gu(j, b):
                if j < 2:
                    w(pe, l1_lo.sem, l1_lo.nth(2 + j, b + 1 if not isinstance(b, int) else min(b + 1, NB - 1)))
                else:
                    pe.wait_ge(gu_ac.sem, gu_ac.nth(j - 2, b))
                for i in range(2):
                    m = i * SK + j
                    ins = three(two(bank[j % 2])[:, i, :],
                                [(gu_h[:, c, m * P:(m + 1) * P], gu_l[:, c, m * P:(m + 1) * P], xt_h[3][:, c, :], xt_l[3][:, c, :]) for c in range(C2)])
                ins.then_inc(gu_rdy.sem, 1)

            def d_cp(b):
                pe.wait_ge(ch_ok, b + 1)
                for t in range(T2):
                    dst = ps_tr[:, t * E:(t + 1) * E]
                    mm(dst, before16[:, :], chosen[:, t, :], start=True, stop=(t == 0))
                    if t:
                        mm(dst, ones16[:, :], chosen[:, 0, :], start=False, stop=True)
                for t in range(T2):
                    ins = mm(ps_tr[:, T2 * E:(T2 + 1) * E], ones16[:, :], chosen[:, t, :], start=(t == 0), stop=(t == T2 - 1))
                ins.then_inc(cp_rdy, 1)

            def d_dn(t, b):
                w(pe, x2_ok, b + 2 if not isinstance(b, int) else min(b + 2, NB))
                tt = slice(t * P, (t + 1) * P)
                for k in range(SK):
                    if t == 0:
                        pe.wait_ge(ac_lo.sem, ac_lo.nth(k, b))
                    ins = three(two(ps_yo)[:, t, :], [(ac_h[:, k, tt], ac_l[:, k, tt], dn_h[:, k, :], dn_l[:, k, :])],
                                start=(k == 0), stop=(k == SK - 1))
                if t == T2 - 1:
                    ins.then_inc(dn_rdy, 1)

            def first(n, c, m, d):
                if n is not None:
                    b_l0(0, n)
                    b_l0(1, n)
                if d is not None:
                    d_dn(0, d)
                if c is not None:
                    if isinstance(c, int) and c == 0:
                        pe.wait_ge(vp_ev, 2)
                    else:
                        pe.wait_ge(rt_exp, c)
                    transposes(2, c, xn[2])
                if n is not None:
                    b_l0(2, n)
                    b_l0(3, n)
                if c is not None:
                    c_qp(c)
                if d is not None:
                    d_dn(1, d)
                if c is not None:
                    c_am(c)
                if n is not None:
                    b_l1(0, n)
                if c is not None:
                    c_cnt(c)
                if n is not None:
                    b_l1(1, n)
                if c is not None:
                    if n is not None:
                        pe.wait_ge(x1_ok, n + 1)
                    c_lg(0, c)
                if n is not None:
                    b_l1(2, n)
                    b_l1(3, n)
                for r in range(4):
                    if c is not None:
                        if r < 3:
                            c_lg(r + 1, c)
                        c_pt(2 * r, c)
                        c_pt(2 * r + 1, c)
                    if m is not None and r == 1:
                        if c is not None:
                            pe.wait_ge(vc_ok, c + 1)
                        elif n is not None:
                            pe.wait_ge(tr_lo[1], n + 1)
                        transposes(0, m, xn[0])
                    if d is not None and r == 2:
                        if m is not None:
                            pe.wait_ge(tr_lo[0], m + 1)
                        elif c is not None:
                            pe.wait_ge(vc_ok, c + 1)
                        d_cp(d)
                    if n is not None:
                        b_l1(4 + r, n)
                    if c is not None:
                        c_av(r, c)

            def second(n, c, m, d):
                if m is not None:
                    if c is not None:
                        pe.wait_ge(z_ok.sem, z_ok.nth(3, c))
                        pe.wait_ge(pt_lo_ok.sem, pt_lo_ok.nth(6, c))
                    a_q(m)
                if c is not None:
                    if d is not None:
                        pe.wait_ge(pos_ev, d + 1)
                    c_att(c)
                if m is not None:
                    a_kv(m)
                    a_vals(m)
                if c is not None:
                    c_wc(c)
                if m is not None:
                    a_s(m)
                if n is not None:
                    b_l2(0, n)
                if m is not None:
                    a_sv(m)
                if n is not None:
                    b_l2(1, n)
                if c is not None:
                    pe.wait_ge(tr_lo[4], c + 1)
                    transposes(3, c, xr)
                    if m is not None:
                        pe.wait_ge(vp_ev, m + 1)
                    d_route(c)
                    d_gu(0, c)
                    d_gu(1, c)
                if m is not None:
                    if c is not None:
                        pe.wait_ge(tr_lo[3], c + 1)
                    else:
                        pe.wait_ge(tr_lo[0], m + 1)
                    transposes(1, m, xn[1])
                if c is not None:
                    d_gu(2, c)
                    d_gu(3, c)

            pe.wait_ge(consts2, 25)
            pe.wait_ge(setup_lo, 5)
            first(None, None, 0, None)
            second(None, None, 0, None)
            pe.wait_ge(bools_ok, 3)
            first(0, None, 1, None)
            pe.wait_ge(setup_lo, 8)
            second(0, None, 1, None)
            pe.wait_ge(setup_lo, 10)
            first(1, 0, 2, None)
            second(1, 0, 2, None)
            first(2, 1, 3, 0)
            second(2, 1, 3, 0)
            with pe.Fori(3, NB - 1) as n:
                first(n, n - 1, n + 1, n - 2)
                second(n, n - 1, n + 1, n - 2)
            first(NB - 1, NB - 2, None, NB - 3)
            second(NB - 1, NB - 2, None, NB - 3)
            first(None, NB - 1, None, NB - 2)
            second(None, NB - 1, None, NB - 2)
            first(None, None, None, NB - 1)

            pe.wait_ge(x4_ok, NB)
            pe.wait_ge(tr_lo[3], NB)
            pe.wait_ge(pos_ev, NB)
            pe.wait_ge(gu_ac.sem, gu_ac.nth(3, NB - 1))
            pe.wait_ge(ids_f, 1)
            nc.tensor.transpose(ps_yo[:, 0:E], slots_f[:, :], ident[0:E, 0:E]).then_inc(ids_t, 1)

            def rows_turned(e, u):
                pe.wait_ge(e_x[u], (e - u) * (16 // XD) + 16)
                w(pe, e_trl, e - 1)
                for c in range(C2):
                    ins = nc.tensor.transpose(ps_eg[u % 2][:, c * P:(c + 1) * P], xg[u][:, c * P:(c + 1) * P], ident[:, :])
                ins.then_inc(e_tr, 1)

            def down(e, u):
                pe.wait_ge(e_acl, e + 1)
                w(pe, e_y, e - 1)
                three(ps_lg[:, u % 2, 0:D], [(ea_h[u % 2][:, :], ea_l[u % 2][:, :], ew_h[u][:, 2, :], ew_l[u][:, 2, :])]).then_inc(e_dn, 1)

            def expert(e, u):
                if within(e, 1):
                    rows_turned(e + 1, (u + 1) % XD)
                pe.wait_ge(e_trl, e + 1)
                pe.wait_ge(e_wl, e + 1)
                w(pe, e_ac, e - 1)
                for g_ in range(2):
                    cc = slice(g_ * IE, (g_ + 1) * IE)
                    ins = three(bank[u % 2][:, g_ * P:(g_ + 1) * P],
                                [(ew_h[u][:, c, cc], ew_l[u][:, c, cc], eg_h[u % 2][:, c, :], eg_l[u % 2][:, c, :]) for c in range(C2)])
                ins.then_inc(e_gu, 1)
                if within(e, -1):
                    down(e - 1, (u - 1) % XD)

            rows_turned(0, 0)
            each_expert(pe, expert)
            down(E - 1, (E - 1) % XD)

        @block.vector
        def _(dve):
            v = nc.vector
            ln_chain = [Steps(dve, ln_dve[i], 10 if i else 3) for i in range(4)]

            def plain(site):
                v.memset(dve_pad[:, site:site + 1], 0.0)

            cch = Steps(dve, c_dve, 5)
            rch = Steps(dve, rt_dve, 11)

            def split_low(ks):
                for k in ks:
                    src, landed, hi, lo = splits[k]
                    dve.wait_ge(setup_hi, k + 1)
                    if hi is None:
                        for h in range(HC):
                            hs = slice(h * DH, (h + 1) * DH)
                            last = v.scalar_tensor_tensor(wkr_l[:, :, hs], landed, WS, wkr_h[:, :, hs], ALU.mult, ALU.subtract)
                        last.then_inc(setup_lo, 1)
                    else:
                        v.scalar_tensor_tensor(lo, landed, WS, hi, ALU.mult, ALU.subtract).then_inc(setup_lo, 1)

            setup = Steps(dve, setup_dve, 13)

            def do(ins):
                setup.did(ins)

            def fold_gates():
                dve.wait_ge(small_dma, 16 * 9)
                dve.wait_ge(gates_tanh, 1)
                setup.start(0)
                do(v.tensor_scalar(sg[:, :], raw[:, 4:6], 0.0, None, ALU.is_gt))
                do(v.tensor_scalar(ab[:, :], raw[:, 4:6], 0.0, None, ALU.is_lt))
                setup.wait()
                do(v.tensor_tensor(sg[:, :], sg[:, :], ab[:, :], ALU.subtract))
                setup.wait()
                do(v.tensor_tensor(ab[:, :], raw[:, 4:6], sg[:, :], ALU.mult))
                setup.wait()
                do(v.tensor_tensor(sc[:, 4:5], ab[:, 0:1], ab[:, 1:2], ALU.mult))
                do(v.tensor_tensor(sc[:, 5:6], tg[:, 2:3], raw[:, 6:7], ALU.mult))
                setup.wait()
                do(v.scalar_tensor_tensor(F0, sc[:, 4:5], 8.0 / HS, sc[:, 5:6], ALU.mult, ALU.mult))
                do(v.tensor_copy(G0X, tg[:, 0:1]))
                do(v.tensor_scalar(G1X, tg[:, 1:2], 1 / WS, None, ALU.mult))
                do(v.tensor_scalar(G1F, tg[:, 3:4], 0.5 / WS, None, ALU.mult))
                do(v.tensor_scalar(sc[:, 6:7], sg[:, 1:2], 2.0 * HS, None, ALU.mult))
                do(v.tensor_scalar(sc[:, 7:8], tg[:, 3:4], 1 / WS, None, ALU.mult))
                setup.wait()

            def from_bools(k):
                dve.wait_ge(bools_in[k], 16)
                if k == 0:
                    do(v.tensor_tensor(wb0[:, :, :], byte_rows(0)[:, 0:C2, :], byte_rows(0)[:, C2:4, :], ALU.subtract))
                    setup.wait()
                    ins = v.tensor_scalar(wb0[:, :, :], wb0[:, :, :], sg[:, 0:1], None, ALU.mult)
                    setup.end()
                elif k == 1:
                    ins = v.tensor_scalar(wb1[:, :, :], byte_rows(1), 0.5, sc[:, 6:7], ALU.subtract, ALU.mult)
                else:
                    ins = v.tensor_scalar(wb2[:, :, :], byte_rows(2), 2.0, 1.0, ALU.mult, ALU.subtract)
                ins.then_inc(bools_ok, 1)


            def ln_sums(i, b, src, made, each=1):
                w(dve, ln_nm[i], b)
                dve.wait_ge(made, each * b + each)
                ln_chain[i].start(b)
                for t in range(T2):
                    last = v.bn_stats(stats[i][:, t, :], src[:, t, :])
                ln_chain[i].did(last)

            def ln_guess(i):
                ch = ln_chain[i]
                half = nt[i][:, 0, :]
                ch.wait()
                plain(8 + i)
                for t in range(T2):
                    last = v.bn_aggr(mv[i][:, t, :], stats[i][:, t, :])
                ch.did(last)
                ch.wait()
                ch.did(v.tensor_scalar(half, mv[i][:, :, 1], EPS, -0.5, ALU.add, ALU.mult))
                ch.wait()
                last = v.tensor_scalar(rs[i][:, :].bitcast(I32), half.bitcast(I32), -0.5, GUESS, ALU.mult, ALU.add)
                if i:
                    ch.did(last)
                else:
                    last.then_inc(ln_st, 1)
                    ch.end()

            def ln_coef(i, between=()):
                between = list(between)
                ch = ln_chain[i]
                y, half, step = rs[i], nt[i][:, 0, :], nt[i][:, 1, :]
                for _ in range(3):
                    if between:
                        between.pop(0)()
                    ch.wait()
                    for k in range(T2):
                        last = v.scalar_tensor_tensor(step[:, k:k + 1], y[:, k:k + 1], y[:, k:k + 1], half[:, k:k + 1],
                                                      ALU.mult, ALU.mult)
                    ch.did(last)
                    ch.wait()
                    ch.did(v.scalar_tensor_tensor(y[:, :], step, 1.5, y[:, :], ALU.add, ALU.mult))
                ch.wait()
                v.scalar_tensor_tensor(nb[i][:, :], mv[i][:, :, 0], -1.0, y[:, :], ALU.mult, ALU.mult).then_inc(ln_cf[i], 1)
                ch.end()

            def ln_first(b):
                ln_sums(0, b, x0, x_in, 16)
                ln_guess(0)

            def tr_low(i, b, lo, hi):
                dve.wait_ge(tr_hi[i], b + 1)
                v.tensor_tensor(lo[:, :, :], two(ps_turned[i]), hi[:, :, :], ALU.subtract).then_inc(tr_lo[i], 1)

            def a_v(b):
                dve.wait_ge(v_rdy, b + 1)
                w(dve, vr_ev, b)
                v.scalar_tensor_tensor(v32[:, :], ps_pt0[0:S2, 0:D], 1 / WS, bv[0:S2, :], ALU.mult, ALU.add).then_inc(v_ev, 1)

            def a_l(b):
                dve.wait_ge(s_ev, b + 1)
                w(dve, sv_rdy, b)
                v.tensor_tensor(l32[:, :], s32[:, :], mT[:, :], ALU.add).then_inc(l_ok, 1)

            def a_x1(b):
                dve.wait_ge(sv_ev, b + 1)
                w(dve, x1_copied, b)
                w(dve, ln_nm[1], b)
                v.scalar_tensor_tensor(x1[:, :, :], o32[:, :, :], G0X, x0[:, :, :], ALU.mult, ALU.add).then_inc(x1_ok, 1)

            def b_lo(hi, lo, hh, hl, j, b):
                dve.wait_ge(hi.sem, hi.nth(j, b))
                v.scalar_tensor_tensor(hl[:, 2 * j:2 * j + 2, :], two(bank[j % 2]), 0.0, hh[:, 2 * j:2 * j + 2, :],
                                       ALU.max, ALU.subtract).then_inc(lo.sem, 1)

            def b_l0(j, b):
                b_lo(l0_hi, l0_lo, h0_h, h0_l, j, b)

            def b_l1(j, b):
                b_lo(l1_hi, l1_lo, h1_h, h1_l, j, b)

            def b_x2(b):
                dve.wait_ge(l2_rdy, b + 1)
                dve.wait_ge(x1_copied, b + 1)
                w(dve, x3_ok, b)
                w(dve, ln_nm[2], b)
                v.scalar_tensor_tensor(x2[:, :, :], two(ps_yo), F0, x1_kept[:, :, :], ALU.mult, ALU.add).then_inc(x2_ok, 1)

            def c_qp(b):
                dve.wait_ge(qp_hi, b + 1)
                v.scalar_tensor_tensor(qp_l[:, :, :], two(ps_m), 1 / WS, qp_h[:, :, :], ALU.mult, ALU.subtract).then_inc(qp_lo, 1)

            def c_argmax(b):
                dve.wait_ge(am_rdy, b + 1)
                cch.start(b)
                plain(1)
                for t in range(T2):
                    last = v.max(am8[:, t, :], ps_tr[:, t * S2:(t + 1) * S2])
                cch.did(last)
                cch.wait()
                plain(2)
                for t in range(T2):
                    last = v.max_index(ami[:, t, :], am8[:, t, :], ps_tr[:, t * S2:(t + 1) * S2])
                cch.did(last)
                cch.wait()
                cch.did(v.tensor_copy(amf[:, :], ami[:, :, 0]))
                cch.wait()
                for t in range(T2):
                    last = v.tensor_scalar(hot[:, t, :], iota_k[:, :], amf[:, t:t + 1], None, ALU.is_equal)
                last.then_inc(hot_ok, 1)

            def c_counts(b):
                dve.wait_ge(cnt_rdy, b + 1)
                v.tensor_scalar(mrow[:, :, :], ps_tr[:, 2 * P:2 * P + S2].unsqueeze(1).to_broadcast([P, HB, S2]),
                                0.0, NEG, ALU.is_equal, ALU.mult).then_inc(mrow_ok, 1)
                cch.did(v.tensor_copy(cnt[:, :], ps_tr[0:S2, 3 * P:3 * P + 1]))
                cch.wait()
                v.tensor_copy(vc_h[:, DH:VW], cnt[:, :])
                dve.wait_ge(handoff, b + 1)
                cch.did(v.tensor_scalar(vc[:, :], vpc[:, :], cnt[:, 0:1], None, ALU.mult))
                cch.wait()
                v.tensor_copy(vc_h[:, 0:DH], vc[:, :]).then_inc(av_dve, 1)
                dve.wait_ge(av_dve, 5 * b + 1)
                v.tensor_tensor(vc_l[:, 0:DH], vc[:, :], vc_h[:, 0:DH], ALU.subtract).then_inc(vc_ok, 1)
                cch.end()

            def c_max(r, b):
                dve.wait_ge(lg_rdy.sem, lg_rdy.nth(r, b))
                lg = ps_lg[:, :, 0:HB * S2].rearrange("p g (h k) -> p g h k", k=S2)
                if r:
                    dve.wait_ge(p_ok.sem, p_ok.nth(r - 1, b))
                else:
                    w(dve, p_ok.sem, p_ok.nth(3, b - 1))
                v.tensor_reduce(rmax[:, :].rearrange("p (g h) -> p g h", g=2), lg, AX, ALU.max).then_inc(mx_dve, 1)
                dve.wait_ge(mx_dve, 4 * b + r + 1)
                v.tensor_tensor(z[:, :, :].rearrange("p (g h) k -> p g h k", g=2), lg,
                                rmax[:, :].rearrange("p (g h) -> p g h", g=2).unsqueeze(3).to_broadcast([P, 2, HB, S2]),
                                ALU.subtract).then_inc(z_ok.sem, 1)

            def c_pt(k, b):
                dve.wait_ge(pt_hi_ok.sem, pt_hi_ok.nth(k, b))
                hh = slice(k % 2 * HB, (k % 2 + 1) * HB)
                v.tensor_tensor(pt_l[:, hh, :], ps_pt[k % 2][0:S2, :].rearrange("p (h n) -> p h n", h=HB),
                                pt_h[:, hh, :], ALU.subtract).then_inc(pt_lo_ok.sem, 1)

            def c_norm(r, b):
                t, c = divmod(r, C2)
                dve.wait_ge(av_rdy.sem, av_rdy.nth(r, b))
                av = ps_m[:, 0:HC * VW].rearrange("p (h n) -> p h n", n=VW)
                v.reciprocal(rden[:, :], av[:, :, DH]).then_inc(av_dve, 1)
                dve.wait_ge(av_dve, 5 * b + r + 2)
                v.tensor_tensor(att[:, t, c * P:(c + 1) * P].rearrange("p (h n) -> p h n", n=DH), av[:, :, 0:DH],
                                rden[:, :].unsqueeze(2).to_broadcast([P, HC, DH]), ALU.mult).then_inc(av_ev.sem, 1)

            def c_x3(b):
                dve.wait_ge(wc_rdy, b + 1)
                w(dve, x4_ok, b)
                v.scalar_tensor_tensor(x3[:, :, :], two(ps_m), G1X, x2[:, :, :], ALU.mult, ALU.add).then_inc(x3_ok, 1)

            def d_max(b):
                dve.wait_ge(rt_rdy, b + 1)
                plain(3)
                for t in range(T2):
                    last = v.max(lt8[:, t, :], ps_pt0[:, t * (E + 1):t * (E + 1) + E])
                last.then_inc(lt_ok, 1)
                dve.wait_ge(lt_ok, b + 1)
                v.tensor_scalar(ltm[:, :], lt8[:, :, 0], -1 / WS, None, ALU.mult).then_inc(rt_max, 1)

            def d_choose(b):
                rch.start(b)
                dve.wait_ge(rt_exp, b + 1)
                plain(4)
                for t in range(T2):
                    last = v.max(e8[:, t, :], ex[:, t, :])
                rch.did(last)
                rch.wait()
                plain(5)
                for t in range(T2):
                    last = v.match_replace(erp[:, t, :], e8[:, t, :], ex[:, t, :], -1.0)
                rch.did(last)
                rch.did(v.tensor_reduce(es8[:, :], e8[:, :, :], AX, ALU.add))
                rch.wait()
                rch.did(v.reciprocal(er8[:, :], es8[:, :]))
                rch.did(v.tensor_scalar(chosen[:, :, :], erp[:, :, :], 0.0, None, ALU.is_lt))
                rch.wait()
                w(dve, xr_out, 16 * b)
                for t in range(T2):
                    last = v.scalar_tensor_tensor(xr[:, t, D:XR], ex[:, t, :], er8[:, t:t + 1], chosen[:, t, :], ALU.mult, ALU.mult)
                last.then_inc(ch_ok, 1)

            def d_pos(b):
                dve.wait_ge(cp_rdy, b + 1)
                rch.did(v.tensor_tensor(pos[:, :, :], ps_tr[:, 0:T2 * E].rearrange("p (t e) -> p t e", t=T2),
                                        carry[:, :].unsqueeze(1).to_broadcast([P, T2, E]), ALU.add))
                rch.wait()
                v.tensor_tensor(carry[:, :], ps_tr[:, T2 * E:(T2 + 1) * E], carry[:, :], ALU.add).then_inc(pos_ev, 1)

            def d_slots(b):
                w(dve, scattered, 16 * T2 * TOPK * b)
                rch.did(v.scalar_tensor_tensor(kept[:, :, :], pos[:, :, :], float(CAP), chosen[:, :, :], ALU.is_lt, ALU.mult))
                rch.did(v.tensor_tensor(key[:, :, :], ebase[:, :].unsqueeze(1).to_broadcast([P, T2, E]), pos[:, :, :], ALU.subtract))
                rch.wait()
                rch.did(v.tensor_tensor(val[:, :, :], key[:, :, :], kept[:, :, :], ALU.mult))
                rch.wait()
                plain(6)
                for t in range(T2):
                    last = v.max(v8[:, t, :], val[:, t, :])
                rch.did(last)
                rch.did(v.tensor_scalar(tokf[:, :], tokf[:, :], float(S), None, ALU.add))
                rch.wait()
                v.tensor_copy(toki[:, :], tokf[:, :]).then_inc(tok_ok, 1)
                v.tensor_scalar(slot[:, :, :], v8[:, :, :], -1.0, float(NT), ALU.mult, ALU.add).then_inc(slots_ok, 1)
                rch.end()

            def d_gu(j, b):
                dve.wait_ge(gu_th.sem, gu_th.nth(j, b))
                two_ = two(bank[j % 2])
                v.scalar_tensor_tensor(ga[:, j, :], th[:, j, :], 1.0, two_[:, 0, :], ALU.add, ALU.mult).then_inc(gu_dve, 1)
                dve.wait_ge(gu_dve, 4 * b + j + 1)
                v.scalar_tensor_tensor(ac[:, j, :], ga[:, j, :], 0.5 / (WS * WS), two_[:, 1, :], ALU.mult, ALU.mult).then_inc(gu_ac.sem, 1)

            def d_ac(j, b):
                dve.wait_ge(ac_hi.sem, ac_hi.nth(j, b))
                v.tensor_tensor(ac_l[:, j, :], ac[:, j, :], ac_h[:, j, :], ALU.subtract).then_inc(ac_lo.sem, 1)

            def d_x4(b):
                dve.wait_ge(dn_rdy, b + 1)
                w(dve, x4_out, 16 * b)
                v.tensor_scalar(sgc[:, :], sgt[:, :], 1.0, G1F, ALU.add, ALU.mult).then_inc(sg_ok, 1)
                dve.wait_ge(sg_ok, b + 1)
                for t in range(T2):
                    last = v.scalar_tensor_tensor(x4[:, t, :], two(ps_yo)[:, t, :], sgc[:, t:t + 1], x3[:, t, :], ALU.mult, ALU.add)
                last.then_inc(x4_ok, 1)

            def first(n, c, m, d):
                if n is not None:
                    b_l0(0, n)
                    b_l0(1, n)
                if c is not None:
                    tr_low(2, c, xt_l[2], xt_h[2])
                if n is not None:
                    b_l0(2, n)
                    b_l0(3, n)
                if c is not None:
                    c_qp(c)
                if c is not None:
                    c_argmax(c)
                if d is not None:
                    d_x4(d)
                if c is not None:
                    c_counts(c)
                if d is not None:
                    d_choose(d)
                if n is not None:
                    b_l1(0, n)
                if c is not None:
                    c_max(0, c)
                if m is not None:
                    ln_first(m)
                if n is not None:
                    b_l1(1, n)
                for r in range(4):
                    if m is not None and r == 2:
                        tr_low(0, m, xt_l[0], xt_h[0])
                    if c is not None:
                        if r < 3:
                            c_max(r + 1, c)
                        c_pt(2 * r, c)
                        c_pt(2 * r + 1, c)
                    if n is not None and r == 1:
                        b_l1(2, n)
                    if c is not None:
                        c_norm(r, c)
                    if d is not None and r == 2:
                        d_pos(d)
                if n is not None:
                    b_l1(3, n)
                if d is not None:
                    d_slots(d)

            def second(n, c, m, d):
                if c is not None:
                    tr_low(4, c, at_l, at_h)
                if m is not None:
                    a_v(m)
                if c is not None:
                    c_x3(c)
                    ln_sums(3, c, x3, x3_ok)
                    ln_guess(3)
                if m is not None:
                    a_l(m)
                if c is not None:
                    ln_coef(3)

                def beside_second_norm():
                    parts = []
                    if c is not None:
                        parts.append(lambda: tr_low(3, c, xt_l[3], xt_h[3]))
                    if n is not None:
                        parts.append(lambda: b_x2(n))
                        parts.append(lambda: ln_sums(2, n, x2, x2_ok))
                    return parts

                if m is not None:
                    a_x1(m)
                    ln_sums(1, m, x1, x1_ok)
                    ln_guess(1)
                    ln_coef(1, beside_second_norm())
                else:
                    for part in beside_second_norm():
                        part()
                if c is not None:
                    d_gu(0, c)
                if n is not None:
                    ln_guess(2)
                if c is not None:
                    d_gu(1, c)
                if m is not None:
                    tr_low(1, m, xt_l[1], xt_h[1])
                if c is not None:
                    d_max(c)
                    d_ac(0, c)
                beside = [] if c is None else [lambda: d_gu(2, c), lambda: d_ac(1, c), lambda: d_gu(3, c)]
                if n is not None:
                    ln_coef(2, beside)
                else:
                    for part in beside:
                        part()
                if c is not None:
                    d_ac(2, c)
                    d_ac(3, c)

            ln_first(0)
            split_low(FOR_A)
            fold_gates()
            from_bools(0)
            from_bools(1)
            dve.wait_ge(consts2, 25)
            tr_low(0, 0, xt_l[0], xt_h[0])
            second(None, None, 0, None)
            from_bools(2)
            split_low(FOR_C)
            first(0, None, 1, None)
            second(0, None, 1, None)
            split_low(FOR_D)
            first(1, 0, 2, None)
            second(1, 0, 2, None)
            first(2, 1, 3, 0)
            second(2, 1, 3, 0)
            with dve.Fori(3, NB - 1) as n:
                first(n, n - 1, n + 1, n - 2)
                second(n, n - 1, n + 1, n - 2)
            first(NB - 1, NB - 2, None, NB - 3)
            second(NB - 1, NB - 2, None, NB - 3)
            first(None, NB - 1, None, NB - 2)
            second(None, NB - 1, None, NB - 2)
            first(None, None, None, NB - 1)

            dve.wait_ge(ids_in, 16)
            v.tensor_copy(slots_f[:, :], slots_row[:, :]).then_inc(ids_f, 1)
            dve.wait_ge(ids_t, 1)
            v.tensor_copy(ids[:, :], ps_yo[:, 0:E]).then_inc(ids_ok, 1)
            dve.wait_ge(ids_ok, 1)

            def gather_ids(e, u):
                w(dve, e_tr, e - XD + 1)
                v.tensor_copy(gid[u][:, :], ids[:, bass.ds(e, 1)]).then_inc(e_gid, 1)

            def split_weights(e, u):
                dve.wait_ge(e_wh, e + 1)
                v.scalar_tensor_tensor(ew_l[u][:, :, :], ew[u % 2][:, :, :], WS, ew_h[u][:, :, :], ALU.mult, ALU.subtract).then_inc(e_wl, 1)

            def rows_low(e, u):
                dve.wait_ge(e_trh, e + 1)
                v.tensor_scalar(ewt[u][:, :], xg[u][:, bass.ds(D + e, 1)], sc[:, 7:8], None, ALU.mult).then_inc(e_wt, 1)
                v.tensor_tensor(eg_l[u % 2][:, :, :], ps_eg[u % 2][:, 0:D].rearrange("p (c n) -> p c n", c=C2), eg_h[u % 2][:, :, :],
                                ALU.subtract).then_inc(e_trl, 1)

            def weighted(e, u):
                dve.wait_ge(e_wt, e + 1)
                dve.wait_ge(e_dn, e + 1)
                w(dve, e_out, 16 * (e - 1))
                v.tensor_copy(aid[u][:, :], ids[:, bass.ds(e, 1)]).then_inc(e_aid, 1)
                v.tensor_scalar(ey[u % 2][:, :], ps_lg[:, u % 2, 0:D], ewt[u][:, 0:1], None, ALU.mult).then_inc(e_y, 1)

            def expert(e, u):
                if within(e, XD - 1):
                    gather_ids(e + XD - 1, (u - 1) % XD)
                if within(e, 1):
                    rows_low(e + 1, (u + 1) % XD)
                dve.wait_ge(e_th, e + 1)
                v.scalar_tensor_tensor(ega[u % 2][:, :], eth[u % 2][:, :], 1.0, bank[u % 2][:, 0:P], ALU.add, ALU.mult).then_inc(e_ga, 1)
                dve.wait_ge(e_ga, e + 1)
                v.scalar_tensor_tensor(eac[u % 2][:, :], ega[u % 2][:, :], 0.5 / (WS * WS), bank[u % 2][:, P:2 * P], ALU.mult, ALU.mult).then_inc(e_ac, 1)
                if within(e, -1):
                    weighted(e - 1, (u - 1) % XD)
                dve.wait_ge(e_ach, e + 1)
                v.tensor_tensor(ea_l[u % 2][:, :], eac[u % 2][:, :], ea_h[u % 2][:, :], ALU.subtract).then_inc(e_acl, 1)
                if within(e, 2):
                    split_weights(e + 2, (u + 2) % XD)

            for e in range(XD - 1):
                gather_ids(e, e)
            split_weights(0, 0)
            split_weights(1, 1)
            rows_low(0, 0)
            each_expert(dve, expert)
            weighted(E - 1, (E - 1) % XD)


def kernel(**inputs):
    from concourse import bacc as _bacc
    from concourse.bass_utils import run_bass_kernel_spmd as _run

    a = {k: np.asarray(v) for k, v in inputs.items()}
    f = {
        "x": a["x"],
        "ctxT": a["ctx_1024"].transpose(0, 2, 1),
        "maskT": a["mask_1xSxS2_ff0"][0].T,
        "g_xattn": a["g_xattn"], "g_ffn": a["g_ffn"],
        "wq0": a["L0_xattn_kernel_q"][0, 0], "wk0": a["L0_xattn_kernel_k"][0, 0], "wv0": a["L0_xattn_kernel_v"][0, 0],
        "bq0": a["L0_xattn_bias_q"].reshape(C2, P).T, "bk0": a["L0_xattn_bias_k"].reshape(C2, P).T, "bv0": a["L0_xattn_bias_v"],
        "k0": a["L0_ffn_k0"].view(np.int32), "k1": a["L0_ffn_k1"].view(np.int32), "k2": a["L0_ffn_k2"].view(np.int32),
        "s0": a["L0_ffn_s0"].reshape(1), "s1": a["L0_ffn_s1"].reshape(1), "s2": a["L0_ffn_s2"].reshape(1),
        "wqT1": a["L1_xattn_Wq"].T, "wkvT1": a["L1_xattn_Wkv"].T, "wcT1": a["L1_xattn_Wc"].T,
        "gates_w": np.concatenate([a["L1_ffn_gate_w"], a["L1_ffn_shared_gate_w"]], axis=1),
        "sgu_w": a["L1_ffn_shared_gate_up_w"], "sdown_w": a["L1_ffn_shared_down_w"],
        "egu_w": a["L1_ffn_expert_gate_up_w"], "edown_w": a["L1_ffn_expert_down_w"],
    }
    nc = _bacc.Bacc("TRN2", target_bir_lowering=False, num_devices=1)
    arrays, args = {}, []
    for name, v in f.items():
        v = np.ascontiguousarray(v)
        arrays[f"in_{name}"] = v
        args.append(nc.dram_tensor(f"in_{name}", v.shape, mybir.dt.from_np(v.dtype), kind="ExternalInput").ap())
    out = nc.dram_tensor("out_0", [NT + CAP, D], F32, kind="ExternalOutput").ap()
    xrows = nc.dram_tensor("xrows", [NT, XR], F32, kind="Internal").ap()
    table = nc.dram_tensor("table", [E * CAP, 1], I32, kind="Internal").ap()
    build(nc, *args, out, xrows, table)
    r = _run(nc, [arrays], core_ids=[0])
    return r.results[0]["out_0"][:NT].reshape(NB, S, D)
```
